# Optimizing a Trainium2 kernel written in Bass

```python
import numpy as np
import jax
import jax.numpy as jnp

def _softmax(x, axis=-1):
    return jax.nn.softmax(x, axis=axis)

def _gelu(x):
    return jax.nn.gelu(x, approximate=True)

def _silu(x):
    return jax.nn.silu(x)

def _sigmoid(x):
    return jax.nn.sigmoid(x)

def _layernorm(x, axis=-1, eps=1e-05):
    m = jnp.mean(x, axis=axis, keepdims=True)
    v = jnp.var(x, axis=axis, keepdims=True)
    return (x - m) / jnp.sqrt(v + eps)

def _scatter_add(tgt, idx, src, axis=0):
    return tgt.at[idx].add(src)

def _segment_sum(src, seg, n):
    return jax.ops.segment_sum(src, seg, n)
kernel_name = 'mk_seq_preln_d1_jaxref_r8_c0f7f3'

def setup_inputs(seed: int=0):
    np.random.seed(seed)
    _w = jnp.asarray

    def _L0_attn_setup():
        import jax, jax.numpy as jnp
        import numpy as np
        NEG_BIG = -1e+38

        def _wkv_scan(w, u, k, v, aa0, bb0, pp0):
            kT = jnp.moveaxis(k, 1, 0)
            vT = jnp.moveaxis(v, 1, 0)

            def step(carry, kv):
                aa, bb, pp = carry
                kt, vt = kv
                ww = u + kt
                p = jnp.maximum(pp, ww)
                e1 = jnp.exp(pp - p)
                e2 = jnp.exp(ww - p)
                y = (e1 * aa + e2 * vt) / (e1 * bb + e2)
                ww2 = pp + w
                p2 = jnp.maximum(ww2, kt)
                e1 = jnp.exp(ww2 - p2)
                e2 = jnp.exp(kt - p2)
                return ((e1 * aa + e2 * vt, e1 * bb + e2, p2), y)
            (aa, bb, pp), yT = jax.lax.scan(step, (aa0, bb0, pp0), (kT, vT))
            return (jnp.moveaxis(yT, 0, 1), aa, bb, pp)

        def _reference_tuple_inner(x, W_rvk, W_out, time_decay, time_first):
            B, T, C = x.shape
            rvk = jnp.einsum('btc,dc->btd', x, W_rvk)
            r, v, k = jnp.split(rvk, 3, axis=-1)
            w = -jnp.exp(time_decay)
            u = time_first
            aa0 = jnp.zeros((B, C), dtype=x.dtype)
            bb0 = jnp.zeros((B, C), dtype=x.dtype)
            pp0 = jnp.full((B, C), NEG_BIG, dtype=x.dtype)
            wkv, aa, bb, pp = _wkv_scan(w, u, k, v, aa0, bb0, pp0)
            rwkv = jax.nn.sigmoid(r) * wkv
            out = jnp.einsum('btc,dc->btd', rwkv, W_out)
            h = aa
            c = jnp.stack([bb, pp], axis=-1).reshape(B, 2 * C)
            return (out, h, c)
        key = jax.random.key(seed)
        k1, k2, k3 = jax.random.split(key, 3)
        B, T, C = (32, 128, 128)
        x = jax.random.normal(k1, (B, T, C), dtype=jnp.float32)
        W_rvk = jax.random.normal(k2, (3 * C, C), dtype=jnp.float32) * (1.0 / np.sqrt(C))
        W_out = jax.random.normal(k3, (C, C), dtype=jnp.float32) * (1.0 / np.sqrt(C))
        time_decay = jnp.ones((C,), dtype=jnp.float32)
        time_first = jnp.ones((C,), dtype=jnp.float32)
        return {'x': x, 'W_rvk': W_rvk, 'W_out': W_out, 'time_decay': time_decay, 'time_first': time_first}
    _L0_attn_in = _L0_attn_setup()

    def _L0_ffn_setup():
        import jax, jax.numpy as jnp
        import numpy as np
        DIM = 128
        DEPTH = 6
        HEADS = 16
        DIM_HEAD = 64
        WINDOW = 32
        INNER = HEADS * DIM_HEAD
        DIM_INNER = int(DIM * 4 * 2 / 3)
        QK_SCALE = 8.0

        def shift_tokens(t):
            a, s = jnp.split(t, 2, -1)
            s = jnp.pad(s, ((0, 0), (1, 0), (0, 0)))[:, :-1]
            return jnp.concatenate([a, s], -1)

        def l2norm(t):
            return t / jnp.maximum(jnp.linalg.norm(t, axis=-1, keepdims=True), 1e-12)

        def rotate_half(x):
            x1, x2 = jnp.split(x, 2, -1)
            return jnp.concatenate([-x2, x1], -1)

        def rotary_tables(n):
            half = jnp.arange(0, DIM_HEAD, 2, dtype=jnp.float32)
            inv_freq = 1.0 / 10000.0 ** (half / DIM_HEAD)
            t = jnp.arange(n, dtype=jnp.float32)
            freqs = t[:, None] * inv_freq[None, :]
            freqs = jnp.concatenate([freqs, freqs], -1)
            base_scale = (half + 0.4 * DIM_HEAD) / (1.4 * DIM_HEAD)
            power = (t - n // 2) / (WINDOW // 2)
            scale = base_scale[None, :] ** power[:, None]
            scale = jnp.concatenate([scale, scale], -1)
            return (freqs, scale)

        def local_attention(q, k, v):
            b, h, n, d = q.shape
            w = WINDOW
            nw = n // w
            bq = q.reshape(b, h, nw, w, d)
            bk = k.reshape(b, h, nw, w, d)
            bv = v.reshape(b, h, nw, w, d)

            def look(t):
                p = jnp.pad(t, ((0, 0), (0, 0), (1, 0), (0, 0), (0, 0)))
                return jnp.concatenate([p[:, :, :nw], p[:, :, 1:]], axis=3)
            bk2, bv2 = (look(bk), look(bv))
            seq = jnp.arange(n).reshape(nw, w)
            seq_p = jnp.pad(seq, ((1, 0), (0, 0)), constant_values=-1)
            jt = jnp.concatenate([seq_p[:nw], seq_p[1:]], axis=1)
            it = seq[:, :, None]
            jb = jt[:, None, :]
            mask = (it < jb) | (it > jb + w) | (jb == -1)
            sim = jnp.einsum('bhwie,bhwje->bhwij', bq, bk2) * QK_SCALE
            sim = jnp.where(mask, -jnp.finfo(sim.dtype).max, sim)
            attn = jax.nn.softmax(sim, -1)
            out = jnp.einsum('bhwij,bhwje->bhwie', attn, bv2)
            return out.reshape(b, h, n, d)

        def attn_layer(x, Wqkv, qs, ksc, Wo):
            b, n, _ = x.shape
            qkv = x @ Wqkv
            q, k, v = jnp.split(qkv, 3, -1)
            sh = lambda t: t.reshape(b, n, HEADS, DIM_HEAD).transpose(0, 2, 1, 3)
            q, k, v = (sh(q), sh(k), sh(v))
            q = l2norm(q) * qs
            k = l2norm(k) * ksc
            freqs, scale = rotary_tables(n)
            cos, sin = (jnp.cos(freqs), jnp.sin(freqs))
            q = q * cos * scale + rotate_half(q) * sin * scale
            inv = 1.0 / scale
            k = k * cos * inv + rotate_half(k) * sin * inv
            out = local_attention(q, k, v)
            out = out.transpose(0, 2, 1, 3).reshape(b, n, INNER)
            return out @ Wo

        def ffn_layer(x, g, bln, W1, b1, W2, b2):
            mu = x.mean(-1, keepdims=True)
            var = ((x - mu) ** 2).mean(-1, keepdims=True)
            xn = (x - mu) / jnp.sqrt(var + 1e-05) * g + bln
            hg = xn @ W1 + b1
            a, gate = jnp.split(hg, 2, -1)
            return a * jax.nn.gelu(gate, approximate=False) @ W2 + b2
        key = jax.random.key(seed)
        ks = jax.random.split(key, 8)
        B, N = (2, 256)
        init = lambda k, shape: jax.random.normal(k, shape, jnp.float32) * 0.02
        return {'x': jax.random.normal(ks[0], (B, N, DIM), jnp.float32), 'Wqkv': init(ks[1], (DEPTH, DIM, 3 * INNER)), 'q_scale': jnp.ones((DEPTH, DIM_HEAD), jnp.float32), 'k_scale': jnp.ones((DEPTH, DIM_HEAD), jnp.float32), 'Wo': init(ks[2], (DEPTH, INNER, DIM)), 'ln_g': jnp.ones((DEPTH, DIM), jnp.float32), 'ln_b': jnp.zeros((DEPTH, DIM), jnp.float32), 'W1': init(ks[3], (DEPTH, DIM, 2 * DIM_INNER)), 'b1': jnp.zeros((DEPTH, 2 * DIM_INNER), jnp.float32), 'W2': init(ks[4], (DEPTH, DIM_INNER, DIM)), 'b2': jnp.zeros((DEPTH, DIM), jnp.float32)}
    _L0_ffn_in = _L0_ffn_setup()
    _d = {'L0_attn_x': _L0_attn_in['x'], 'L0_attn_W_rvk': _L0_attn_in['W_rvk'], 'L0_attn_W_out': _L0_attn_in['W_out'], 'L0_attn_time_decay': _L0_attn_in['time_decay'], 'L0_attn_time_first': _L0_attn_in['time_first'], 'L0_ffn_Wqkv': _L0_ffn_in['Wqkv'], 'L0_ffn_q_scale': _L0_ffn_in['q_scale'], 'L0_ffn_k_scale': _L0_ffn_in['k_scale'], 'L0_ffn_Wo': _L0_ffn_in['Wo'], 'L0_ffn_ln_g': _L0_ffn_in['ln_g'], 'L0_ffn_ln_b': _L0_ffn_in['ln_b'], 'L0_ffn_W1': _L0_ffn_in['W1'], 'L0_ffn_b1': _L0_ffn_in['b1'], 'L0_ffn_W2': _L0_ffn_in['W2'], 'L0_ffn_b2': _L0_ffn_in['b2']}
    _x0 = _d['L0_attn_x']
    _d['L0_attn_x'] = jax.random.normal(jax.random.fold_in(jax.random.key(seed), 1), (4, 512, 128), dtype=_x0.dtype)
    del _x0
    return _d

def reference(L0_attn_x, L0_attn_W_rvk, L0_attn_W_out, L0_attn_time_decay, L0_attn_time_first, L0_ffn_Wqkv, L0_ffn_q_scale, L0_ffn_k_scale, L0_ffn_Wo, L0_ffn_ln_g, L0_ffn_ln_b, L0_ffn_W1, L0_ffn_b1, L0_ffn_W2, L0_ffn_b2):

    def _L0_attn_ref(x, W_rvk, W_out, time_decay, time_first):
        import jax, jax.numpy as jnp
        import numpy as np
        NEG_BIG = -1e+38

        def _wkv_scan(w, u, k, v, aa0, bb0, pp0):
            kT = jnp.moveaxis(k, 1, 0)
            vT = jnp.moveaxis(v, 1, 0)

            def step(carry, kv):
                aa, bb, pp = carry
                kt, vt = kv
                ww = u + kt
                p = jnp.maximum(pp, ww)
                e1 = jnp.exp(pp - p)
                e2 = jnp.exp(ww - p)
                y = (e1 * aa + e2 * vt) / (e1 * bb + e2)
                ww2 = pp + w
                p2 = jnp.maximum(ww2, kt)
                e1 = jnp.exp(ww2 - p2)
                e2 = jnp.exp(kt - p2)
                return ((e1 * aa + e2 * vt, e1 * bb + e2, p2), y)
            (aa, bb, pp), yT = jax.lax.scan(step, (aa0, bb0, pp0), (kT, vT))
            return (jnp.moveaxis(yT, 0, 1), aa, bb, pp)

        def _reference_tuple_inner(x, W_rvk, W_out, time_decay, time_first):
            B, T, C = x.shape
            rvk = jnp.einsum('btc,dc->btd', x, W_rvk)
            r, v, k = jnp.split(rvk, 3, axis=-1)
            w = -jnp.exp(time_decay)
            u = time_first
            aa0 = jnp.zeros((B, C), dtype=x.dtype)
            bb0 = jnp.zeros((B, C), dtype=x.dtype)
            pp0 = jnp.full((B, C), NEG_BIG, dtype=x.dtype)
            wkv, aa, bb, pp = _wkv_scan(w, u, k, v, aa0, bb0, pp0)
            rwkv = jax.nn.sigmoid(r) * wkv
            out = jnp.einsum('btc,dc->btd', rwkv, W_out)
            h = aa
            c = jnp.stack([bb, pp], axis=-1).reshape(B, 2 * C)
            return (out, h, c)
        return _reference_tuple_inner(x, W_rvk, W_out, time_decay, time_first)[0]

    def _L0_ffn_ref(x, Wqkv, q_scale, k_scale, Wo, ln_g, ln_b, W1, b1, W2, b2):
        import jax, jax.numpy as jnp
        import numpy as np
        DIM = 128
        DEPTH = 6
        HEADS = 16
        DIM_HEAD = 64
        WINDOW = 32
        INNER = HEADS * DIM_HEAD
        DIM_INNER = int(DIM * 4 * 2 / 3)
        QK_SCALE = 8.0

        def shift_tokens(t):
            a, s = jnp.split(t, 2, -1)
            s = jnp.pad(s, ((0, 0), (1, 0), (0, 0)))[:, :-1]
            return jnp.concatenate([a, s], -1)

        def l2norm(t):
            return t / jnp.maximum(jnp.linalg.norm(t, axis=-1, keepdims=True), 1e-12)

        def rotate_half(x):
            x1, x2 = jnp.split(x, 2, -1)
            return jnp.concatenate([-x2, x1], -1)

        def rotary_tables(n):
            half = jnp.arange(0, DIM_HEAD, 2, dtype=jnp.float32)
            inv_freq = 1.0 / 10000.0 ** (half / DIM_HEAD)
            t = jnp.arange(n, dtype=jnp.float32)
            freqs = t[:, None] * inv_freq[None, :]
            freqs = jnp.concatenate([freqs, freqs], -1)
            base_scale = (half + 0.4 * DIM_HEAD) / (1.4 * DIM_HEAD)
            power = (t - n // 2) / (WINDOW // 2)
            scale = base_scale[None, :] ** power[:, None]
            scale = jnp.concatenate([scale, scale], -1)
            return (freqs, scale)

        def local_attention(q, k, v):
            b, h, n, d = q.shape
            w = WINDOW
            nw = n // w
            bq = q.reshape(b, h, nw, w, d)
            bk = k.reshape(b, h, nw, w, d)
            bv = v.reshape(b, h, nw, w, d)

            def look(t):
                p = jnp.pad(t, ((0, 0), (0, 0), (1, 0), (0, 0), (0, 0)))
                return jnp.concatenate([p[:, :, :nw], p[:, :, 1:]], axis=3)
            bk2, bv2 = (look(bk), look(bv))
            seq = jnp.arange(n).reshape(nw, w)
            seq_p = jnp.pad(seq, ((1, 0), (0, 0)), constant_values=-1)
            jt = jnp.concatenate([seq_p[:nw], seq_p[1:]], axis=1)
            it = seq[:, :, None]
            jb = jt[:, None, :]
            mask = (it < jb) | (it > jb + w) | (jb == -1)
            sim = jnp.einsum('bhwie,bhwje->bhwij', bq, bk2) * QK_SCALE
            sim = jnp.where(mask, -jnp.finfo(sim.dtype).max, sim)
            attn = jax.nn.softmax(sim, -1)
            out = jnp.einsum('bhwij,bhwje->bhwie', attn, bv2)
            return out.reshape(b, h, n, d)

        def attn_layer(x, Wqkv, qs, ksc, Wo):
            b, n, _ = x.shape
            qkv = x @ Wqkv
            q, k, v = jnp.split(qkv, 3, -1)
            sh = lambda t: t.reshape(b, n, HEADS, DIM_HEAD).transpose(0, 2, 1, 3)
            q, k, v = (sh(q), sh(k), sh(v))
            q = l2norm(q) * qs
            k = l2norm(k) * ksc
            freqs, scale = rotary_tables(n)
            cos, sin = (jnp.cos(freqs), jnp.sin(freqs))
            q = q * cos * scale + rotate_half(q) * sin * scale
            inv = 1.0 / scale
            k = k * cos * inv + rotate_half(k) * sin * inv
            out = local_attention(q, k, v)
            out = out.transpose(0, 2, 1, 3).reshape(b, n, INNER)
            return out @ Wo

        def ffn_layer(x, g, bln, W1, b1, W2, b2):
            mu = x.mean(-1, keepdims=True)
            var = ((x - mu) ** 2).mean(-1, keepdims=True)
            xn = (x - mu) / jnp.sqrt(var + 1e-05) * g + bln
            hg = xn @ W1 + b1
            a, gate = jnp.split(hg, 2, -1)
            return a * jax.nn.gelu(gate, approximate=False) @ W2 + b2
        for i in range(DEPTH):
            x = attn_layer(shift_tokens(x), Wqkv[i], q_scale[i], k_scale[i], Wo[i]) + x
            x = ffn_layer(shift_tokens(x), ln_g[i], ln_b[i], W1[i], b1[i], W2[i], b2[i]) + x
        return x
    x = L0_attn_x
    x = x + _L0_attn_ref(_layernorm(x, axis=-1), L0_attn_W_rvk, L0_attn_W_out, L0_attn_time_decay, L0_attn_time_first)
    x = x + _L0_ffn_ref(_layernorm(x, axis=-1), L0_ffn_Wqkv, L0_ffn_q_scale, L0_ffn_k_scale, L0_ffn_Wo, L0_ffn_ln_g, L0_ffn_ln_b, L0_ffn_W1, L0_ffn_b1, L0_ffn_W2, L0_ffn_b2)
    return x

_drawn_inputs = setup_inputs


def setup_inputs(seed=0):
    import zlib

    import numpy as np

    out = dict(_drawn_inputs(seed))
    spreads = {'L0_attn_time_decay': (1.0, 0.6),
     'L0_attn_time_first': (1.0, 0.578),
     'L0_ffn_q_scale': (1.0, 0.6),
     'L0_ffn_k_scale': (1.0, 0.6),
     'L0_ffn_ln_g': (1.0, 0.6),
     'L0_ffn_ln_b': (0.0, 0.8),
     'L0_ffn_b1': (0.0, 0.8),
     'L0_ffn_b2': (0.0, 0.1)}
    factors = {'L0_ffn_W1': 3.819, 'L0_ffn_W2': 3.743}
    for name, (base, spread) in spreads.items():
        noise = np.random.default_rng([zlib.crc32(name.encode()), seed]).standard_normal(out[name].shape)
        drawn = base * np.exp(spread * noise) if base else spread * noise
        out[name] = jnp.asarray(drawn.astype(out[name].dtype))
    for name, factor in factors.items():
        out[name] = (out[name] * factor).astype(out[name].dtype)
    return out
```

```python
from contextlib import ExitStack

import numpy as np

import concourse.bass as bass
from concourse import mybir

F32 = mybir.dt.float32
F32R = mybir.dt.float32r
BF16 = mybir.dt.bfloat16
I32 = mybir.dt.int32
ALU = mybir.AluOpType
ACT = mybir.ActivationFunctionType
AX = mybir.AxisListType

P = 128
BATCH, SEQ = 4, 512
DEPTH, HEADS, DH, WINDOW = 6, 16, 64, 32
INNER = HEADS * DH
NBLK = SEQ // P
NWIN = P // WINDOW
ITEMS = DEPTH * BATCH
BLOCKS = ITEMS * NBLK
CHUNK = 512
HPC = CHUNK // DH
QK_CHUNKS = 2 * INNER // CHUNK
V_CHUNKS = 2 * (INNER // CHUNK)
CHUNKS = QK_CHUNKS + V_CHUNKS
W_CHUNKS = 3 * INNER // CHUNK
PAIRS = HEADS // 2
DIM_INNER = int(P * 4 * 2 / 3)
HID = [P, P, DIM_INNER - 2 * P]
NHID = len(HID)
QK_SCALE = 8.0
EPS = 1e-5
NEG_BIG = -1e38
MASKED = -1e30
DVE_FIRST, DVE_BODY = 80, 100


def shape_constants():
    ident = np.eye(P, dtype=np.float32)
    center = (np.eye(P) - 1.0 / P).astype(np.float32)
    half = np.arange(0, DH, 2, dtype=np.float32)
    inv_freq = (1.0 / np.float32(10000.0) ** (half / np.float32(DH))).astype(np.float32)
    t = np.arange(SEQ, dtype=np.float32)
    freqs = t[:, None] * inv_freq[None, :]
    base = (half + np.float32(0.4 * DH)) / np.float32(1.4 * DH)
    power = (t - SEQ // 2) / np.float32(WINDOW // 2)
    scale = base[None, :].astype(np.float64) ** power[:, None]
    cos, sin = np.cos(freqs.astype(np.float64)), np.sin(freqs.astype(np.float64))
    rot = np.stack([
        np.concatenate([cos * scale, cos * scale], -1),
        np.concatenate([-sin * scale, sin * scale], -1),
        np.concatenate([cos / scale, cos / scale], -1),
        np.concatenate([-sin / scale, sin / scale], -1),
    ])
    rot = np.ascontiguousarray(rot.reshape(4, NBLK, P, DH).transpose(2, 0, 1, 3)).astype(np.float32)
    q = np.arange(P)[:, None] % WINDOW
    j = np.arange(2 * WINDOW)[None, :]
    own = np.where((j >= q) & (j <= q + WINDOW), 0.0, MASKED)
    first = np.where(j < WINDOW, MASKED, own)
    mask = np.stack([
        np.concatenate([first if w == 0 else own for _ in range(2) for w in range(NWIN)], -1),
        np.concatenate([own for _ in range(2) for w in range(NWIN)], -1),
    ]).transpose(1, 0, 2)
    return {"ident": ident, "center": center, "rot": rot,
            "mask": np.ascontiguousarray(mask.astype(np.float32))}


def need(eng, sem, value):
    if isinstance(value, int) and value <= 0:
        return
    eng.wait_ge(sem, value)


def rsqrt(eng, seq, x, y, tmp, tmp_i):
    seq(eng.tensor_scalar(tmp_i, x.bitcast(I32), 1, None, ALU.logical_shift_right))
    seq(eng.tensor_scalar(y.bitcast(I32), tmp_i, -1.0, float(0x5F3759DF), ALU.mult, ALU.add))
    for newton in range(3):
        seq(eng.tensor_tensor(tmp, x, y, ALU.mult))
        seq(eng.scalar_tensor_tensor(tmp, tmp, -0.5, y, ALU.mult, ALU.mult))
        last = eng.scalar_tensor_tensor(y, tmp, 1.5, y, ALU.add, ALU.mult)
        if newton < 2:
            seq(last)
    return last


class Chain:

    def __init__(self, eng, sem, base=0):
        self.eng, self.sem, self.count, self.base = eng, sem, 0, base

    def __call__(self, instruction):
        instruction.then_inc(self.sem, 1)
        self.count += 1
        self.eng.wait_ge(self.sem, self.base + self.count)


def build(nc, x, w_rvk, w_out, time_decay, time_first, w_qkv, q_scale, k_scale, w_o, ln_g, ln_b,
          w_1, b_1, w_2, b_2, ident_in, center_in, rot_in, mask_in, out):
    x_res_dram = nc.dram_tensor("x_res_scratch", (P, BATCH, SEQ), F32, kind="Internal").ap()
    with ExitStack() as whole:
        def sb(name, shape, dt=F32, ctx=whole):
            return ctx.enter_context(nc.sbuf_tensor(name, shape, dt))

        def sem(name, ctx=whole):
            return ctx.enter_context(nc.semaphore(name))

        bank = [whole.enter_context(nc.psum_tensor(f"bank{i}", [P, 512], F32)) for i in range(8)]

        ident = sb("ident", [P, P])
        center = sb("center", [P, P])
        mean_col = sb("mean_col", [P, 1])
        x_state = sb("x_state", [P, BATCH, SEQ])
        vecs = sb("vecs", [P, 2 * NHID + 3, DEPTH])
        B1_UP, B1_GATE, B2, LN_G, LN_B = 0, NHID, 2 * NHID, 2 * NHID + 1, 2 * NHID + 2
        qk_rows = sb("qk_rows", [P, DEPTH, 4, DH])
        rot = sb("rot", [P, 4, NBLK, DH])
        mask_bf = sb("mask_bf", [P, 2, 512], BF16)
        ident_bf = sb("ident_bf", [P, P], BF16)

        time_mixing(nc, sb, sem, bank, x, w_rvk, w_out, time_decay, time_first, q_scale, k_scale,
                    ln_g, ln_b, b_1, b_2, ident_in, center_in, rot_in, mask_in, ident, center,
                    mean_col, x_state, vecs, qk_rows, rot, mask_bf, ident_bf, x_res_dram)
        transformer(nc, bank, w_qkv, w_o, w_1, w_2, ident, center, mean_col, x_state, vecs,
                    qk_rows, rot, mask_bf, ident_bf, (B1_UP, B1_GATE, B2, LN_G, LN_B))
        finish(nc, bank, ident, x_state, x_res_dram, out)


def time_mixing(nc, sb_, sem_, bank, x, w_rvk, w_out, time_decay, time_first, q_scale, k_scale,
                ln_g, ln_b, b_1, b_2, ident_in, center_in, rot_in, mask_in, ident, center,
                mean_col, x_state, vecs, qk_rows, rot, mask_bf, ident_bf, x_res_dram):
    with ExitStack() as ctx:
        def sb(name, shape, dt=F32):
            return ctx.enter_context(nc.sbuf_tensor("mix_" + name, shape, dt))

        def sem(name):
            return ctx.enter_context(nc.semaphore(name))

        x_nat = sb("x_nat", [P, BATCH * NBLK, P])
        w_rvk_nat = sb("w_rvk_nat", [P, 3, P])
        w_out_nat = sb("w_out_nat", [P, P])
        w_rvk_t = sb("w_rvk_t", [P, 3, P])
        w_out_t = sb("w_out_t", [P, P])
        decay = sb("decay", [P, 1])
        first = sb("first", [P, 1])
        exp_decay = sb("exp_decay", [P, 1])
        w_neg = sb("w_neg", [P, 1])
        vec_rows = sb("vec_rows", [DEPTH * (2 * NHID + 3), P])
        mask_f = sb("mask_f", [P, 2, 512])
        stats = sb("stats", [P, NBLK, 6])
        mv = sb("mv", [P, NBLK, 2])
        var = sb("var", [P, NBLK])
        rstd = sb("rstd", [P, NBLK])
        rstd2 = sb("rstd2", [P, NBLK])
        nt, nti = sb("nt", [P, NBLK]), sb("nti", [P, NBLK], I32)
        xn = sb("xn", [P, NBLK, P])
        xn_t, x_t = sb("xn_t", [P, SEQ]), sb("x_t", [P, SEQ])
        k_s, v_s, er = sb("k_s", [P, SEQ]), sb("v_s", [P, SEQ]), sb("er", [P, SEQ])
        pp = sb("pp", [P, SEQ + 1])
        aa = sb("aa", [P, SEQ + 1])
        bb = sb("bb", [P, SEQ + 1])
        d1, d2 = sb("d1", [P, SEQ]), sb("d2", [P, SEQ])
        e1, e2, e2v = sb("e1", [P, SEQ]), sb("e2", [P, SEQ]), sb("e2v", [P, SEQ])
        pk, g1, g2 = sb("pk", [P, SEQ]), sb("g1", [P, SEQ]), sb("g2", [P, SEQ])
        f1, f2 = sb("f1", [P, SEQ]), sb("f2", [P, SEQ])
        f1a, f2v, f1b = sb("f1a", [P, SEQ]), sb("f2v", [P, SEQ]), sb("f1b", [P, SEQ])
        num, den, rden = sb("num", [P, SEQ]), sb("den", [P, SEQ]), sb("rden", [P, SEQ])
        rwkv = sb("rwkv", [P, SEQ])
        x_res = sb("x_res", [P, SEQ])
        xc, xsq = sb("xc", [P, SEQ]), sb("xsq", [P, SEQ])

        loaded_x, loaded_w, loaded_t, stored = (sem(s) for s in
                                                ("a_loaded_x", "a_loaded_w", "a_loaded_t", "a_stored"))
        dve_seq, rows_clear, loaded_v, v_turned, v_copied = (sem(s) for s in (
            "a_dve_seq", "a_rows_clear", "a_loaded_v", "a_v_turned", "a_v_copied"))
        w_t_ready, w_t_evac = sem("a_w_t_ready"), sem("a_w_t_evac")
        exp_dec = sem("a_exp_dec")
        xn_ready, xt_ready, xt_evac = sem("a_xn_ready"), sem("a_xt_ready"), sem("a_xt_evac")
        rvk_ready, rvk_evac = sem("a_rvk_ready"), sem("a_rvk_evac")
        d_ready, e_ready = sem("a_d_ready"), sem("a_e_ready")
        g_ready, f_ready = sem("a_g_ready"), sem("a_f_ready")
        rwkv_ready, o_ready, res_ready = sem("a_rwkv_ready"), sem("a_o_ready"), sem("a_res_ready")
        cen_ready, cen_evac = sem("a_cen_ready"), sem("a_cen_evac")
        st_ready, rs_ready, bc_ready, xl_ready = (sem(s) for s in
                                                  ("a_st_ready", "a_rs_ready", "a_bc_ready", "a_xl_ready"))
        block = ctx.enter_context(nc.Block())

        @block.sync
        def _(sp):
            sp.dma_start(ident[:], ident_in).then_inc(loaded_x, 16)
            sp.dma_start(x_nat[:], x.rearrange("b (j p) c -> p (b j) c", p=P)).then_inc(loaded_x, 16)
            sp.dma_start(w_rvk_nat[:], w_rvk.rearrange("(j p) c -> p j c", p=P)).then_inc(loaded_w, 16)
            sp.dma_start(w_out_nat[:], w_out).then_inc(loaded_w, 16)
            sp.dma_start(center[:], center_in).then_inc(loaded_w, 16)
            sp.dma_start(decay[:], time_decay.rearrange("(p a) -> p a", a=1)).then_inc(loaded_w, 16)
            sp.dma_start(first[:], time_first.rearrange("(p a) -> p a", a=1)).then_inc(loaded_w, 16)
            sp.dma_start(mask_f[:], mask_in).then_inc(loaded_t, 16)
            sp.dma_start(rot[:], rot_in).then_inc(loaded_t, 16)
            n_t = 2
            h = DH // 2
            for kind, src in ((0, q_scale), (2, k_scale)):
                rows = qk_rows[:, :, kind, :]
                swap = qk_rows[:, :, kind + 1, :]
                for dst, s in ((rows, src), (swap[:, :, 0:h], src[:, h:DH]), (swap[:, :, h:DH], src[:, 0:h])):
                    sp.dma_start(dst, s.rearrange("(o l) d -> o l d", o=1).to_broadcast(
                        [P, DEPTH, s.shape[1]])).then_inc(loaded_t, 16)
                    n_t += 1
            sp.wait_ge(rows_clear, 1)
            for c, src in ((2 * NHID, b_2), (2 * NHID + 1, ln_g), (2 * NHID + 2, ln_b)):
                sp.dma_start(vec_rows[DEPTH * c:DEPTH * (c + 1), :], src).then_inc(loaded_v, 16)
            for part in range(2):
                for j in range(NHID):
                    lo, c = part * DIM_INNER + j * P, part * NHID + j
                    sp.dma_start(vec_rows[DEPTH * c:DEPTH * (c + 1), 0:HID[j]],
                                 b_1[:, lo:lo + HID[j]]).then_inc(loaded_v, 16)
            for b in range(BATCH):
                sp.wait_ge(res_ready, b + 1)
                sp.dma_start(x_res_dram[:, b, :], x_res[:]).then_inc(stored, 16)
            sp.wait_ge(stored, 16 * BATCH)
            sp.wait_ge(loaded_t, 16 * n_t)

        @block.vector
        def _(dve):
            seq = Chain(dve, dve_seq)
            dve.memset(vec_rows[:], 0.0).then_inc(rows_clear, 1)
            seq(dve.memset(mean_col[:], 1.0 / P))
            seq(dve.memset(pp[:, 0:1], NEG_BIG))
            seq(dve.memset(aa[:, 0:1], 0.0))
            seq(dve.memset(bb[:, 0:1], 0.0))
            dve.wait_ge(exp_dec, 1)
            seq(dve.tensor_scalar(w_neg[:], exp_decay[:], -1.0, None, ALU.mult))
            dve.wait_ge(loaded_x, 32)
            seq(dve.tensor_copy(ident_bf[:], ident[:]))
            for b in range(BATCH):
                for j in range(NBLK):
                    seq(dve.bn_stats(stats[:, j, :], x_nat[:, b * NBLK + j, :]))
                for j in range(NBLK):
                    seq(dve.bn_aggr(mv[:, j, :], stats[:, j, :]))
                seq(dve.tensor_scalar(var[:], mv[:, :, 1], EPS, None, ALU.add))
                seq(rsqrt(dve, seq, var[:], rstd[:], nt[:], nti[:]))
                need(dve, xt_ready, 2 * b)
                for j in range(NBLK):
                    dve.tensor_scalar(xn[:, j, :], x_nat[:, b * NBLK + j, :], mv[:, j, 0:1],
                                      rstd[:, j:j + 1], ALU.subtract, ALU.mult).then_inc(xn_ready, 1)
                dve.wait_ge(rvk_evac, 3 * b + 3)
                need(dve, e_ready, 2 * b)
                need(dve, f_ready, 2 * b)
                seq(dve.tensor_tensor_scan(pp[:, 1:], w_neg[:].to_broadcast([P, SEQ]), k_s[:],
                                           NEG_BIG, ALU.add, ALU.max))
                prev = pp[:, 0:SEQ]
                dve.scalar_tensor_tensor(d1[:], prev, w_neg[:], pp[:, 1:], ALU.add,
                                         ALU.subtract).then_inc(d_ready, 1)
                dve.tensor_tensor(d2[:], k_s[:], pp[:, 1:], ALU.subtract).then_inc(d_ready, 1)
                seq(dve.scalar_tensor_tensor(pk[:], k_s[:], first[:], prev, ALU.add, ALU.max))
                dve.tensor_tensor(g1[:], prev, pk[:], ALU.subtract).then_inc(g_ready, 1)
                dve.scalar_tensor_tensor(g2[:], k_s[:], first[:], pk[:], ALU.add,
                                         ALU.subtract).then_inc(g_ready, 1)
                dve.wait_ge(e_ready, 2 * b + 2)
                seq(dve.tensor_tensor(e2v[:], e2[:], v_s[:], ALU.mult))
                seq(dve.tensor_tensor_scan(aa[:, 1:], e1[:], e2v[:], 0.0, ALU.mult, ALU.add))
                seq(dve.tensor_tensor_scan(bb[:, 1:], e1[:], e2[:], 0.0, ALU.mult, ALU.add))
                dve.wait_ge(f_ready, 2 * b + 2)
                seq(dve.tensor_tensor(f1a[:], f1[:], aa[:, 0:SEQ], ALU.mult))
                seq(dve.tensor_tensor(f1b[:], f1[:], bb[:, 0:SEQ], ALU.mult))
                seq(dve.tensor_tensor(f2v[:], f2[:], v_s[:], ALU.mult))
                seq(dve.tensor_tensor(num[:], f1a[:], f2v[:], ALU.add))
                seq(dve.tensor_tensor(den[:], f1b[:], f2[:], ALU.add))
                seq(dve.scalar_tensor_tensor(den[:], er[:], 1.0, den[:], ALU.add, ALU.mult))
                seq(dve.reciprocal(rden[:], den[:]))
                need(dve, o_ready, b)
                dve.tensor_tensor(rwkv[:], num[:], rden[:], ALU.mult).then_inc(rwkv_ready, 1)
                dve.wait_ge(o_ready, b + 1)
                need(dve, stored, 16 * b)
                need(dve, cen_ready, b)
                dve.tensor_tensor(x_res[:], bank[5][:], x_t[:], ALU.add).then_inc(res_ready, 1)
                dve.wait_ge(st_ready, b + 1)
                seq(dve.tensor_scalar(var[:], bank[7][:, 0:NBLK], EPS, None, ALU.add))
                need(dve, bc_ready, b)
                rsqrt(dve, seq, var[:], rstd2[:], nt[:], nti[:]).then_inc(rs_ready, 1)
                dve.wait_ge(bc_ready, b + 1)
                dve.wait_ge(cen_evac, 2 * b + 2)
                dve.tensor_tensor(x_state[:, b, :], bank[2][:], xc[:], ALU.mult).then_inc(xl_ready, 1)
            dve.wait_ge(loaded_t, 32)
            seq(dve.tensor_copy(mask_bf[:], mask_f[:]))
            dve.wait_ge(v_turned, 1)
            dve.tensor_copy(vecs[:].rearrange("p c l -> p (c l)"),
                            bank[0][:, 0:DEPTH * (2 * NHID + 3)]).then_inc(v_copied, 1)
            dve.wait_ge(v_copied, 1)
            dve.wait_ge(xl_ready, BATCH)

        @block.scalar
        def _(act):
            act.wait_ge(loaded_w, 80)
            act.activation(exp_decay[:], decay[:], ACT.Exp).then_inc(exp_dec, 1)
            act.wait_ge(w_t_ready, 1)
            act.copy(w_rvk_t[:].rearrange("p j c -> p (j c)"), bank[0][:, 0:3 * P]).then_inc(w_t_evac, 1)
            act.copy(w_out_t[:], bank[0][:, 3 * P:4 * P]).then_inc(w_t_evac, 1)
            for b in range(BATCH):
                act.wait_ge(xt_ready, 2 * b + 1)
                act.copy(xn_t[:], bank[0][:]).then_inc(xt_evac, 1)
                act.wait_ge(xt_ready, 2 * b + 2)
                need(act, res_ready, b)
                act.copy(x_t[:], bank[1][:]).then_inc(xt_evac, 1)
                act.wait_ge(rvk_ready, 3 * b + 3)
                need(act, rwkv_ready, b)
                act.activation(er[:], bank[2][:], ACT.Exp, scale=-1.0).then_inc(rvk_evac, 1)
                act.copy(v_s[:], bank[3][:]).then_inc(rvk_evac, 1)
                act.copy(k_s[:], bank[4][:]).then_inc(rvk_evac, 1)
                act.wait_ge(d_ready, 2 * b + 1)
                act.activation(e1[:], d1[:], ACT.Exp).then_inc(e_ready, 1)
                act.wait_ge(d_ready, 2 * b + 2)
                act.activation(e2[:], d2[:], ACT.Exp).then_inc(e_ready, 1)
                act.wait_ge(g_ready, 2 * b + 1)
                act.activation(f1[:], g1[:], ACT.Exp).then_inc(f_ready, 1)
                act.wait_ge(g_ready, 2 * b + 2)
                act.activation(f2[:], g2[:], ACT.Exp).then_inc(f_ready, 1)
                act.wait_ge(cen_ready, b + 1)
                need(act, xl_ready, b)
                act.copy(xc[:], bank[6][:]).then_inc(cen_evac, 1)
                act.activation(xsq[:], bank[6][:], ACT.Square).then_inc(cen_evac, 1)

        @block.tensor
        def _(pe):
            pe.wait_ge(loaded_x, 32)
            pe.wait_ge(loaded_w, 80)
            for j in range(3):
                pe.transpose(bank[0][:, j * P:(j + 1) * P], w_rvk_nat[:, j, :], ident[:])
            pe.transpose(bank[0][:, 3 * P:4 * P], w_out_nat[:], ident[:]).then_inc(w_t_ready, 1)
            pe.wait_ge(w_t_evac, 2)
            for b in range(BATCH):
                pe.wait_ge(xn_ready, 4 * b + 4)
                for j in range(NBLK):
                    mm = pe.transpose(bank[0][:, j * P:(j + 1) * P], xn[:, j, :], ident[:])
                mm.then_inc(xt_ready, 1)
                for j in range(NBLK):
                    mm = pe.transpose(bank[1][:, j * P:(j + 1) * P], x_nat[:, b * NBLK + j, :], ident[:])
                mm.then_inc(xt_ready, 1)
                pe.wait_ge(xt_evac, 2 * b + 1)
                need(pe, xl_ready, b)
                for j in range(3):
                    pe.matmul(bank[2 + j][:], w_rvk_t[:, j, :], xn_t[:], start=True,
                              stop=True).then_inc(rvk_ready, 1)
                pe.wait_ge(rwkv_ready, b + 1)
                pe.matmul(bank[5][:], w_out_t[:], rwkv[:], start=True, stop=True).then_inc(o_ready, 1)
                pe.wait_ge(res_ready, b + 1)
                pe.matmul(bank[6][:], center[:], x_res[:], start=True, stop=True).then_inc(cen_ready, 1)
                pe.wait_ge(cen_evac, 2 * b + 2)
                for j in range(NBLK):
                    mm = pe.matmul(bank[7][:, j:j + 1], xsq[:, j * P:(j + 1) * P], mean_col[:],
                                   start=True, stop=True)
                mm.then_inc(st_ready, 1)
                pe.wait_ge(rs_ready, b + 1)
                for j in range(NBLK):
                    mm = pe.matmul(bank[2][:, j * P:(j + 1) * P],
                                   rstd2[:, j:j + 1].to_broadcast([P, P]), ident[:], start=True, stop=True)
                mm.then_inc(bc_ready, 1)
            pe.wait_ge(loaded_v, 16 * (3 + 2 * NHID))
            n_vec = DEPTH * (2 * NHID + 3)
            pe.transpose(bank[0][:, 0:n_vec], vec_rows[:], ident[0:n_vec, 0:n_vec]).then_inc(v_turned, 1)


def transformer(nc, bank, w_qkv, w_o, w_1, w_2, ident, center, mean_col, x_state, vecs, qk_rows,
                rot, mask_bf, ident_bf, vec_at):
    B1_UP, B1_GATE, B2, LN_G, LN_B = vec_at
    PAD = WINDOW
    NVEC = 2 * NHID + 3
    N_CONST = 6
    with ExitStack() as ctx:
        def sb(name, shape, dt=F32):
            return ctx.enter_context(nc.sbuf_tensor(name, shape, dt))

        def sem(name):
            return ctx.enter_context(nc.semaphore(name))

        xs = sb("xs", [P, SEQ])
        xs_hi, xs_lo = sb("xs_hi", [P, PAD + SEQ], F32R), sb("xs_lo", [P, PAD + SEQ], F32R)
        w_raw = sb("w_raw", [P, 2, CHUNK])
        w_hi, w_lo = sb("w_hi", [P, 3 * INNER], F32R), sb("w_lo", [P, 3 * INNER], F32R)
        tables = sb("tables", [P, 2, 4, NBLK, DH])
        qk = sb("qk", [P, 2, QK_CHUNKS, CHUNK])
        qk_sin = sb("qk_sin", [P, QK_CHUNKS, CHUNK])
        squares = sb("squares", [P, 2, CHUNK])
        norm2 = sb("norm2", [P, QK_CHUNKS * HPC])
        norm_t, norm_ti = sb("norm_t", [P, QK_CHUNKS * HPC]), sb("norm_ti", [P, QK_CHUNKS * HPC], I32)
        rnorm = sb("rnorm", [P, QK_CHUNKS * HPC])
        q_t = sb("q_t", [P, PAIRS, P])
        k_t = sb("k_t", [P, PAIRS, PAD + SEQ])
        v = sb("v", [P, NBLK, 2, HEADS, DH + 1])
        probs = sb("probs", [P, 2, 2, 512])
        row_max = sb("row_max", [P, 2, HPC])
        p_t = sb("p_t", [P, 2, 4, P])
        row_sum = sb("row_sum", [P, 2, 2, 4])
        o = sb("o", [P, 2, 2, 4, DH])
        o_t = sb("o_t", [P, PAIRS, SEQ])
        w_o_s, w_1_s, w_2_s = sb("w_o_s", [P, PAIRS, P]), sb("w_1_s", [P, 2 * DIM_INNER]), sb("w_2_s", [P, NHID, P])
        vec = sb("vec", [P, NVEC])
        x1, xs2 = sb("x1", [P, SEQ]), sb("xs2", [P, SEQ])
        xc, xsq, xn = sb("xc", [P, SEQ]), sb("xsq", [P, SEQ]), sb("xn", [P, SEQ])
        var, rstd = sb("var", [P, NBLK]), sb("rstd", [P, NBLK])
        var_t, var_ti = sb("var_t", [P, NBLK]), sb("var_ti", [P, NBLK], I32)
        gated, hidden = sb("gated", [P, SEQ]), sb("hidden", [P, NHID, SEQ])

        raw_loaded, tail_w_loaded = [sem("raw_loaded0"), sem("raw_loaded1")], sem("tail_w_loaded")
        chunk_ready, qk_turned, scores_ready = sem("chunk_ready"), sem("qk_turned"), sem("scores_ready")
        p_turned, o_ready, o_turned = sem("p_turned"), sem("o_ready"), sem("o_turned")
        wo_ready, cen_ready, var_ready, rstd_wide = (sem(s) for s in ("wo_ready", "cen_ready", "var_ready", "rstd_wide"))
        gate_ready, up_ready, y_ready = sem("gate_ready"), sem("up_ready"), sem("y_ready")
        chunk_free, qk_evac, exp_ready = sem("chunk_free"), sem("qk_evac"), sem("exp_ready")
        p_evac, o_t_evac = sem("p_evac"), sem("o_t_evac")
        cen_evac, gelu_ready = sem("cen_evac"), sem("gelu_ready")
        xs_ready, rotated, summed, rnorm_ready = (sem(s) for s in ("xs_ready", "rotated", "summed", "rnorm_ready"))
        shifted_ready, o_normed, x1_done, xs2_ready = (sem(s) for s in ("scores_shifted", "o_normed", "x1_done", "xs2_ready"))
        rstd_ready, xn_ready, hidden_ready, x2_done = (sem(s) for s in ("rstd_ready", "xn_ready", "hidden_ready", "x2_done"))
        dve_seq, constants_ready = sem("dve_seq"), sem("constants_ready")
        qk_added, qk_normed, w_split, tables_ready = (sem(s) for s in ("qk_added", "qk_normed", "w_split", "tables_ready"))
        raw_used = sem("raw_used")

        def batch_slot(item):
            if isinstance(item, int):
                return x_state[:, item % BATCH, :]
            return x_state[:, bass.ds(item % BATCH, 1), :].rearrange("p b t -> p (b t)")

        def layer_of(item):
            return item // BATCH

        def steps(item, head, tail, back):
            for t in range(NBLK):
                if t - back >= 0:
                    yield (item, t - back, NBLK * item + t - back) if head else None
                else:
                    yield (item - 1, t - back + NBLK, NBLK * item + t - back) if tail else None

        def run(eng, body):
            body(0, True, False)
            with eng.Fori(1, ITEMS) as item:
                body(item, True, True)
            body(ITEMS, False, True)

        block = ctx.enter_context(nc.Block())

        @block.sync
        def _(sp):
            n_raw = 0
            for layer in range(DEPTH):
                for c in range(W_CHUNKS):
                    if n_raw >= 2:
                        sp.wait_ge(raw_used, n_raw - 1)
                    sp.dma_start(w_raw[:, c % 2, :],
                                 w_qkv[layer, :, c * CHUNK:(c + 1) * CHUNK]).then_inc(raw_loaded[c % 2], 16)
                    n_raw += 1
                    if c == W_CHUNKS - 1:
                        need(sp, x2_done, BATCH * layer)
                        sp.dma_start(w_o_s[:], w_o[layer].rearrange("(p r) n -> r p n", r=P)).then_inc(tail_w_loaded, 16)
                        sp.dma_start(w_1_s[:], w_1[layer]).then_inc(tail_w_loaded, 16)
                        sp.dma_start(w_2_s[:, 0:2, :], w_2[layer, 0:2 * P].rearrange("(j r) n -> r j n", r=P)).then_inc(tail_w_loaded, 16)
                        sp.dma_start(w_2_s[0:HID[2], 2, :], w_2[layer, 2 * P:]).then_inc(tail_w_loaded, 16)

        @block.gpsimd
        def _(pool):
            def raw_arrived(layer, c):
                pool.wait_ge(raw_loaded[c % 2], 16 * (W_CHUNKS // 2) * layer + 16 * (c // 2 + 1))

            def split_weights(layer):
                for c in range(W_CHUNKS):
                    cols = slice(c * CHUNK, (c + 1) * CHUNK)
                    pool.tensor_scalar(w_hi[:, cols], w_raw[:, c % 2, :], 1.0, 0.0, ALU.mult, ALU.add).then_inc(tables_ready, 1)
                    if c + 1 < W_CHUNKS:
                        raw_arrived(layer, c + 1)
                    pool.wait_ge(tables_ready, (W_CHUNKS + 4) * layer + 4 + c + 1)
                    pool.tensor_tensor(w_lo[:, cols], w_raw[:, c % 2, :], w_hi[:, cols].bitcast(F32),
                                       ALU.subtract).then_inc(raw_used, 1)

            def make_tables(layer):
                for kind in range(4):
                    if isinstance(layer, int):
                        dst, row = tables[:, layer % 2, kind, :, :], qk_rows[:, layer, kind, :]
                    else:
                        dst = tables[:, bass.ds(layer % 2, 1), kind, :, :].rearrange("p a t d -> p (a t) d")
                        row = qk_rows[:, bass.ds(layer % DEPTH, 1), kind, :].rearrange("p a d -> p (a d)")
                    pool.tensor_tensor(dst, rot[:, kind, :, :],
                                       row.unsqueeze(1).to_broadcast([P, NBLK, DH]), ALU.mult).then_inc(tables_ready, 1)

            raw_arrived(0, 0)
            make_tables(0)
            split_weights(0)
            pool.wait_ge(raw_used, W_CHUNKS)
            pool.engine_nop().then_inc(w_split, 1)

            def body(item, head, tail):
                for step, now in enumerate(steps(item, head, tail, 0)):
                    if now is None:
                        continue
                    _, t, g = now
                    par = t % 2
                    for c in range(QK_CHUNKS):
                        pool.wait_ge(rotated, QK_CHUNKS * g + c + 1)
                        pool.tensor_tensor(qk[:, par, c, :], qk[:, par, c, :], qk_sin[:, c, :],
                                           ALU.add).then_inc(qk_added, 1)
                    pool.wait_ge(rnorm_ready, g + 1)
                    for c in range(QK_CHUNKS):
                        pool.wait_ge(qk_added, QK_CHUNKS * g + c + 1)
                        view = qk[:, par, c, :].rearrange("p (h d) -> p h d", d=DH)
                        pool.tensor_tensor(view, view, rnorm[:, c * HPC:(c + 1) * HPC].unsqueeze(2)
                                           .to_broadcast([P, HPC, DH]), ALU.mult).then_inc(qk_normed, 1)
                if head:
                    def next_layer(layer):
                        pool.wait_ge(chunk_ready, CHUNKS * NBLK * (item + 1))
                        raw_arrived(layer, 0)
                        make_tables(layer)
                        split_weights(layer)
                        pool.wait_ge(raw_used, W_CHUNKS * (layer + 1))
                    if not isinstance(item, int):
                        with pool.If((item + 1) % BATCH + (item + 1 + 32 - ITEMS) // 32 == 0):
                            next_layer((item + 1) // BATCH)
                        pool.engine_nop().then_inc(w_split, 1)
                    else:
                        pool.engine_nop().then_inc(w_split, 1)

            run(pool, body)

        @block.vector
        def _(dve):
            seq = Chain(dve, dve_seq)

            def make_xs(item, base):
                xb = batch_slot(item)
                half = P // 2
                dve.tensor_copy(xs[0:half, :], xb[0:half, :]).then_inc(dve_seq, 1)
                dve.tensor_copy(xs[half:P, 1:SEQ], xb[half:P, 0:SEQ - 1]).then_inc(dve_seq, 1)
                dve.wait_ge(dve_seq, base + 2)
                dve.tensor_copy(xs_hi[:, PAD:], xs[:]).then_inc(dve_seq, 1)
                dve.wait_ge(dve_seq, base + 3)
                dve.tensor_tensor(xs_lo[:, PAD:], xs[:], xs_hi[:, PAD:].bitcast(F32),
                                  ALU.subtract).then_inc(xs_ready, 1)

            zeros = [xs[:, 0:1], xs_hi[:, 0:PAD].bitcast(F32), xs_lo[:, 0:PAD].bitcast(F32),
                     k_t[:, :, 0:PAD], xs2[:, 0:1]]
            for z in zeros:
                dve.memset(z, 0.0).then_inc(constants_ready, 1)
            dve.memset(v[:, :, :, :, DH:DH + 1], 1.0).then_inc(constants_ready, 1)
            assert len(zeros) + 1 == N_CONST
            dve.wait_ge(constants_ready, N_CONST)
            make_xs(0, 0)
            chained = {}

            def body(item, head, tail):
                seq.count = 0
                first = isinstance(item, int) and item == 0
                seq.base = 3 if first else DVE_FIRST + (item - 1) * DVE_BODY
                stage_a = list(steps(item, head, tail, 0))
                stage_b = list(steps(item, head, tail, 1))
                stage_c = list(steps(item, head, tail, 2))
                for step in range(NBLK):
                    if stage_a[step]:
                        _, t, g = stage_a[step]
                        par = t % 2
                        if t == 0:
                            need(dve, tables_ready, (W_CHUNKS + 4) * layer_of(item) + 4)
                        for c in range(QK_CHUNKS):
                            src = bank[c % 2][:].rearrange("p (h a d) -> p h a d", a=2, d=DH // 2)
                            kind = 2 * (c // 2)

                            def table(k):
                                if isinstance(item, int):
                                    return tables[:, layer_of(item) % 2, k, t, :]
                                return tables[:, bass.ds(layer_of(item) % 2, 1), k, t, :].rearrange("p a d -> p (a d)")

                            dve.wait_ge(chunk_ready, CHUNKS * g + c + 1)
                            need(dve, qk_turned, QK_CHUNKS * (g - 2) + c + 1)
                            dve.tensor_tensor(qk[:, par, c, :].rearrange("p (h d) -> p h d", d=DH),
                                              bank[c % 2][:].rearrange("p (h d) -> p h d", d=DH),
                                              table(kind).unsqueeze(1).to_broadcast([P, HPC, DH]),
                                              ALU.mult).then_inc(dve_seq, 1)
                            seq.count += 1
                            need(dve, qk_added, QK_CHUNKS * (g - 1) + c + 1)
                            dve.tensor_tensor(
                                qk_sin[:, c, :].rearrange("p (h a d) -> p h a d", a=2, d=DH // 2),
                                src[:, :, ::-1, :],
                                table(kind + 1).rearrange("p (a d) -> p a d", a=2).unsqueeze(1)
                                .to_broadcast([P, HPC, 2, DH // 2]), ALU.mult).then_inc(rotated, 1)
                        for c in range(QK_CHUNKS):
                            dve.wait_ge(chunk_free, CHUNKS * g + c + 1)
                            if c == 0:
                                need(dve, qk_normed, QK_CHUNKS * g)
                            dve.tensor_reduce(norm2[:, c * HPC:(c + 1) * HPC],
                                              squares[:, c % 2, :].rearrange("p (h d) -> p h d", d=DH),
                                              AX.X, ALU.add).then_inc(summed, 1)
                        dve.wait_ge(summed, QK_CHUNKS * (g + 1))
                        seq(dve.tensor_scalar(norm2[:], norm2[:], 1e-24, None, ALU.max))
                        rsqrt(dve, seq, norm2[:], rnorm[:], norm_t[:], norm_ti[:]).then_inc(rnorm_ready, 1)
                    if tail and step == 2:
                        m = item - 1
                        if isinstance(m, int):
                            seq(dve.tensor_copy(vec[:], vecs[:, :, layer_of(m)]))
                        else:
                            seq(dve.tensor_copy(vec[:], vecs[:, :, bass.ds(layer_of(m), 1)].rearrange("p c l -> p (c l)")))
                        dve.wait_ge(wo_ready, item)
                        dve.tensor_tensor(x1[:], bank[0][:], batch_slot(m), ALU.add).then_inc(x1_done, 1)
                        dve.wait_ge(x1_done, item)
                        half = P // 2
                        dve.tensor_copy(xs2[0:half, :], x1[0:half, :]).then_inc(xs2_ready, 1)
                        dve.tensor_copy(xs2[half:P, 1:SEQ], x1[half:P, 0:SEQ - 1]).then_inc(xs2_ready, 1)
                    if head and step == NBLK - 1:
                        dve.wait_ge(chunk_ready, CHUNKS * NBLK * (item + 1))
                        make_xs(item + 1, seq.base + seq.count)
                        seq.count += 3
                    if tail and step == NBLK - 1:
                        m = item - 1
                        dve.wait_ge(var_ready, item)
                        seq(dve.tensor_scalar(var[:], bank[0][:, 0:NBLK], EPS, None, ALU.add))
                        rsqrt(dve, seq, var[:], rstd[:], var_t[:], var_ti[:]).then_inc(rstd_ready, 1)
                        dve.wait_ge(rstd_wide, item)
                        dve.wait_ge(cen_evac, 2 * item)
                        seq(dve.scalar_tensor_tensor(xn[:], xc[:], vec[:, LN_G:LN_G + 1], bank[1][:],
                                                     ALU.mult, ALU.mult))
                        dve.tensor_scalar(xn[:], xn[:], vec[:, LN_B:LN_B + 1], None, ALU.add).then_inc(xn_ready, 1)
                    if stage_b[step]:
                        _, t, g = stage_b[step]
                        par = t % 2
                        for r in range(2):
                            view = bank[4 + r][:].rearrange("p (s k) -> p s k", k=2 * WINDOW)
                            dve.wait_ge(scores_ready, 2 * g + r + 1)
                            seq(dve.tensor_reduce(row_max[:, r, :], view, AX.X, ALU.max))
                            need(dve, p_turned, 2 * (g - 2) + r + 1)
                            dve.tensor_tensor(probs[:, par, r, :].rearrange("p (s k) -> p s k", k=2 * WINDOW),
                                              view, row_max[:, r, :].unsqueeze(2).to_broadcast([P, HPC, 2 * WINDOW]),
                                              ALU.subtract).then_inc(shifted_ready, 1)
                    if stage_c[step]:
                        _, t, g = stage_c[step]
                        for mm in range(2):
                            dve.wait_ge(o_ready, 2 * g + mm + 1)
                            for w in range(2):
                                o_bank = bank[6 + w][:, 0:4 * (DH + 1)].rearrange("p (s d) -> p s d", d=DH + 1)
                                dve.reciprocal(row_sum[:, mm, w, :].unsqueeze(2), o_bank[:, :, DH:DH + 1]).then_inc(dve_seq, 1)
                                seq.count += 1
                            dve.wait_ge(dve_seq, seq.base + seq.count)
                            need(dve, o_turned, 2 * (g - 1) + mm + 1)
                            for w in range(2):
                                o_bank = bank[6 + w][:, 0:4 * (DH + 1)].rearrange("p (s d) -> p s d", d=DH + 1)
                                dve.tensor_tensor(o[:, mm, w, :, :], o_bank[:, :, 0:DH],
                                                  row_sum[:, mm, w, :].unsqueeze(2).to_broadcast([P, 4, DH]),
                                                  ALU.mult).then_inc(o_normed, 1)
                    if tail and step == NBLK - 1:
                        m = item - 1
                        for j in range(NHID):
                            dve.wait_ge(gelu_ready, NHID * m + j + 1)
                            dve.wait_ge(up_ready, NHID * m + j + 1)
                            n = HID[j]
                            dve.scalar_tensor_tensor(hidden[0:n, j, :], bank[0][0:n, :], vec[0:n, B1_UP + j:B1_UP + j + 1],
                                                     gated[0:n, :], ALU.add, ALU.mult).then_inc(hidden_ready, 1)
                        dve.wait_ge(y_ready, item)
                        dve.scalar_tensor_tensor(batch_slot(m), bank[0][:], vec[:, B2:B2 + 1], x1[:],
                                                 ALU.add, ALU.add).then_inc(x2_done, 1)
                        dve.wait_ge(x2_done, item)
                chained[(head, tail)] = seq.count

            body(0, True, False)
            assert chained[(True, False)] + 3 == DVE_FIRST, chained
            with dve.Fori(1, ITEMS) as item:
                body(item, True, True)
            assert chained[(True, True)] == DVE_BODY, chained
            body(ITEMS, False, True)

        @block.scalar
        def _(act):
            def body(item, head, tail):
                stage_a = list(steps(item, head, tail, 0))
                stage_b = list(steps(item, head, tail, 1))
                stage_c = list(steps(item, head, tail, 2))
                for step in range(NBLK):
                    if stage_a[step]:
                        _, t, g = stage_a[step]
                        for c in range(QK_CHUNKS):
                            act.wait_ge(rotated, QK_CHUNKS * g + c + 1)
                            need(act, summed, QK_CHUNKS * g + c - 1)
                            act.activation(squares[:, c % 2, :], bank[c % 2][:], ACT.Square).then_inc(chunk_free, 1)
                        for c in range(V_CHUNKS):
                            mm, hh = c // 2, c % 2
                            act.wait_ge(chunk_ready, CHUNKS * g + QK_CHUNKS + c + 1)
                            need(act, o_ready, 2 * (g - NBLK) + mm + 1)
                            act.copy(v[:, t, mm, hh * HPC:(hh + 1) * HPC, 0:DH],
                                     bank[c % 2][:].rearrange("p (h d) -> p h d", d=DH)).then_inc(chunk_free, 1)
                    if tail and step == 2:
                        act.wait_ge(cen_ready, item)
                        act.copy(xc[:], bank[1][:]).then_inc(cen_evac, 1)
                        act.activation(xsq[:], bank[1][:], ACT.Square).then_inc(cen_evac, 1)
                    if stage_b[step]:
                        _, t, g = stage_b[step]
                        for c in range(QK_CHUNKS):
                            act.wait_ge(qk_turned, QK_CHUNKS * g + c + 1)
                            need(act, scores_ready, 2 * g)
                            src = bank[2 + c % 2][:].rearrange("p (h d) -> p h d", d=P)
                            pairs = slice(4 * (c % 2), 4 * (c % 2) + 4)
                            dst = q_t[:, pairs, :] if c < 2 else k_t[:, pairs, PAD + P * t:PAD + P * (t + 1)]
                            act.copy(dst, src).then_inc(qk_evac, 1)
                        for r in range(2):
                            act.wait_ge(shifted_ready, 2 * g + r + 1)
                            act.activation(probs[:, t % 2, r, :], probs[:, t % 2, r, :], ACT.Exp,
                                           scale=QK_SCALE).then_inc(exp_ready, 1)
                    if stage_c[step]:
                        _, t, g = stage_c[step]
                        for r in range(2):
                            act.wait_ge(p_turned, 2 * g + r + 1)
                            need(act, o_ready, 2 * g)
                            act.copy(p_t[:, r, :, :], bank[2 + r][:].rearrange("p (s q) -> p s q", q=P)).then_inc(p_evac, 1)
                        for mm in range(2):
                            act.wait_ge(o_turned, 2 * g + mm + 1)
                            if t == 0 and mm == 0:
                                need(act, wo_ready, item)
                            for w in range(2):
                                cols = P * t + WINDOW * (2 * w + mm)
                                inst = act.copy(o_t[:, :, cols:cols + WINDOW],
                                                bank[2 + mm][:, 256 * w:256 * (w + 1)].rearrange("p (a q) -> p a q", q=WINDOW))
                                inst.then_inc(o_t_evac, 1)
                    if tail and step == NBLK - 1:
                        m = item - 1
                        for j in range(NHID):
                            n = HID[j]
                            act.wait_ge(gate_ready, NHID * m + j + 1)
                            if j > 0:
                                act.wait_ge(hidden_ready, NHID * m + j)
                            act.activation(gated[0:n, :], bank[1][0:n, :], ACT.Gelu,
                                           bias=vec[0:n, B1_GATE + j:B1_GATE + j + 1]).then_inc(gelu_ready, 1)

            run(act, body)

        @block.tensor
        def _(pe):
            def product3(dst, l_hi, l_lo, r_hi, r_lo):
                pe.matmul(dst, l_hi, r_hi, start=True, stop=False)
                pe.matmul(dst, l_hi, r_lo, start=False, stop=False)
                return pe.matmul(dst, l_lo, r_hi, start=False, stop=True)

            def body(item, head, tail):
                stage_a = list(steps(item, head, tail, 0))
                stage_b = list(steps(item, head, tail, 1))
                stage_c = list(steps(item, head, tail, 2))
                blocks_a = lambda step: NBLK * item + step + 1 if head else NBLK * item
                for step in range(NBLK):
                    if stage_a[step]:
                        _, t, g = stage_a[step]
                        if t == 0:
                            pe.wait_ge(xs_ready, item + 1)
                            pe.wait_ge(w_split, item + 1)
                            if isinstance(item, int):
                                pe.wait_ge(constants_ready, N_CONST)
                        if t == NBLK - 1 and tail:
                            pe.wait_ge(x1_done, item)
                            pe.wait_ge(cen_evac, 2 * item)
                        for c in range(CHUNKS):
                            need(pe, chunk_free, CHUNKS * g + c - 1)
                            if c < QK_CHUNKS:
                                at, wc = PAD + P * t, c
                                l_hi, l_lo = xs_hi[:, at:at + P], xs_lo[:, at:at + P]
                            else:
                                m, wc = (c - QK_CHUNKS) // 2, QK_CHUNKS + (c - QK_CHUNKS) % 2
                                at = P * t + WINDOW * m
                                l_hi, l_lo = xs_hi[:, at:at + P], xs_lo[:, at:at + P]
                            cols = slice(wc * CHUNK, (wc + 1) * CHUNK)
                            product3(bank[c % 2][:], l_hi, l_lo, w_hi[:, cols], w_lo[:, cols]).then_inc(chunk_ready, 1)
                    if tail and step == 2:
                        pe.wait_ge(tail_w_loaded, 64 * (layer_of(item - 1) + 1))
                        pe.wait_ge(o_t_evac, 4 * NBLK * item)
                        pe.wait_ge(chunk_free, CHUNKS * blocks_a(step))
                        for p in range(PAIRS):
                            mm = pe.matmul(bank[0][:], w_o_s[:, p, :], o_t[:, p, :], start=(p == 0), stop=(p == PAIRS - 1))
                        mm.then_inc(wo_ready, 1)
                        pe.wait_ge(xs2_ready, 2 * item)
                        pe.matmul(bank[1][:], center[:], xs2[:], start=True, stop=True).then_inc(cen_ready, 1)
                    if tail and step == NBLK - 1:
                        pe.wait_ge(cen_evac, 2 * item)
                        pe.wait_ge(chunk_free, CHUNKS * blocks_a(step))
                        for j in range(NBLK):
                            mm = pe.matmul(bank[0][:, j:j + 1], xsq[:, j * P:(j + 1) * P], mean_col[:], start=True, stop=True)
                        mm.then_inc(var_ready, 1)
                        pe.wait_ge(rstd_ready, item)
                        for j in range(NBLK):
                            mm = pe.matmul(bank[1][:, j * P:(j + 1) * P], rstd[:, j:j + 1].to_broadcast([P, P]), ident[:],
                                           start=True, stop=True)
                        mm.then_inc(rstd_wide, 1)
                    if stage_b[step]:
                        _, t, g = stage_b[step]
                        for c in range(QK_CHUNKS):
                            need(pe, qk_normed, QK_CHUNKS * g + c + 1)
                            if c < 2:
                                need(pe, qk_evac, QK_CHUNKS * g)
                                need(pe, o_t_evac, 4 * (g - 1))
                            else:
                                need(pe, qk_evac, QK_CHUNKS * g + c - 1)
                            for j in range(4):
                                mm = pe.transpose(bank[2 + c % 2][:, j * P:(j + 1) * P],
                                                  qk[:, t % 2, c, j * P:(j + 1) * P], ident[:])
                            mm.then_inc(qk_turned, 1)
                        pe.wait_ge(qk_evac, QK_CHUNKS * (g + 1))
                        for r in range(2):
                            need(pe, shifted_ready, 2 * g + r - 1)
                            s_bank = bank[4 + r]
                            pe.matmul(s_bank[:], ident_bf[:], mask_bf[:, min(t, 1), :], start=True, stop=True)
                            for s in range(2):
                                for slot in range(NWIN):
                                    w = 2 * (slot % 2) + slot // 2
                                    for h in range(4):
                                        pair = 4 * s + h
                                        row = slice(DH * r, DH * (r + 1))
                                        col = (NWIN * s + slot) * 2 * WINDOW
                                        mm = pe.matmul(
                                            s_bank[WINDOW * h:WINDOW * (h + 1), col:col + 2 * WINDOW],
                                            q_t[row, pair, WINDOW * w:WINDOW * (w + 1)],
                                            k_t[row, pair, P * t + WINDOW * w:P * t + WINDOW * w + 2 * WINDOW],
                                            start=False, stop=True, skip_group_check=True)
                            mm.then_inc(scores_ready, 1)
                    if stage_c[step]:
                        _, t, g = stage_c[step]
                        for r in range(2):
                            pe.wait_ge(exp_ready, 2 * g + r + 1)
                            if stage_b[step]:
                                pe.wait_ge(qk_evac, QK_CHUNKS * (g + 2))
                            else:
                                pe.wait_ge(qk_evac, QK_CHUNKS * BLOCKS)
                                pe.wait_ge(o_t_evac, 4 * g)
                            for j in range(4):
                                mm = pe.transpose(bank[2 + r][:, j * P:(j + 1) * P],
                                                  probs[:, t % 2, r, j * P:(j + 1) * P], ident[:])
                            mm.then_inc(p_turned, 1)
                        for m in range(2):
                            pe.wait_ge(constants_ready, N_CONST)
                            pe.wait_ge(p_evac, 2 * (g + 1))
                            if m == 0:
                                need(pe, o_normed, 4 * g)
                            for w in range(2):
                                row = slice(2 * WINDOW * w, 2 * WINDOW * (w + 1))
                                for s in range(2):
                                    for r in range(2):
                                        for h in range(4):
                                            head_no = 8 * s + 2 * h + r
                                            quad = 2 * s + r
                                            mm = pe.matmul(
                                                bank[6 + w][WINDOW * h:WINDOW * (h + 1), quad * (DH + 1):(quad + 1) * (DH + 1)],
                                                p_t[row, r, 2 * s + m, WINDOW * h:WINDOW * (h + 1)],
                                                v[row, t, m, head_no, :], start=True, stop=True)
                            mm.then_inc(o_ready, 1)
                            pe.wait_ge(o_normed, 4 * g + 2 * m + 2)
                            for w in range(2):
                                for s in range(2):
                                    mm = pe.transpose(bank[2 + m][:, (2 * w + s) * P:(2 * w + s + 1) * P],
                                                      o[:, m, w, 2 * s:2 * s + 2, :].rearrange("p r d -> p (r d)"), ident[:])
                            mm.then_inc(o_turned, 1)
                    if tail and step == NBLK - 1:
                        pe.wait_ge(xn_ready, item)
                        for j in range(NHID):
                            if j > 0:
                                pe.wait_ge(hidden_ready, NHID * (item - 1) + j)
                            n = HID[j]
                            gate = DIM_INNER + j * P
                            pe.matmul(bank[1][0:n, :], w_1_s[:, gate:gate + n], xn[:], start=True, stop=True).then_inc(gate_ready, 1)
                            pe.matmul(bank[0][0:n, :], w_1_s[:, j * P:j * P + n], xn[:], start=True, stop=True).then_inc(up_ready, 1)
                        pe.wait_ge(hidden_ready, NHID * item)
                        for j in range(NHID):
                            n = HID[j]
                            mm = pe.matmul(bank[0][:], w_2_s[0:n, j, :], hidden[0:n, j, :], start=(j == 0), stop=(j == NHID - 1))
                        mm.then_inc(y_ready, 1)
                        pe.wait_ge(x2_done, item)

            run(pe, body)



def finish(nc, bank, ident, x_state, x_res_dram, out):
    with ExitStack() as ctx:
        x_res = ctx.enter_context(nc.sbuf_tensor("f_x_res", [P, BATCH, SEQ], F32))
        total = ctx.enter_context(nc.sbuf_tensor("f_total", [P, BATCH, SEQ], F32))
        o_nat = ctx.enter_context(nc.sbuf_tensor("f_o_nat", [P, BATCH, NBLK, P], F32))
        loaded, added, turned, copied, stored = (ctx.enter_context(nc.semaphore(s)) for s in (
            "f_loaded", "f_added", "f_turned", "f_copied", "f_stored"))
        block = ctx.enter_context(nc.Block())

        @block.sync
        def _(sp):
            for b in range(BATCH):
                sp.dma_start(x_res[:, b, :], x_res_dram[:, b, :]).then_inc(loaded, 16)
            for b in range(BATCH):
                sp.wait_ge(copied, b + 1)
                sp.dma_start(out[b].rearrange("(j p) c -> p j c", p=P), o_nat[:, b, :, :]).then_inc(stored, 16)
            sp.wait_ge(stored, 16 * BATCH)

        @block.vector
        def _(dve):
            dve.wait_ge(loaded, 16 * BATCH)
            for b in range(BATCH):
                dve.tensor_tensor(total[:, b, :], x_res[:, b, :], x_state[:, b, :], ALU.add).then_inc(added, 1)

        @block.tensor
        def _(pe):
            for b in range(BATCH):
                pe.wait_ge(added, b + 1)
                for j in range(NBLK):
                    mm = pe.transpose(bank[b][:, j * P:(j + 1) * P], total[:, b, j * P:(j + 1) * P], ident[:])
                mm.then_inc(turned, 1)

        @block.scalar
        def _(act):
            for b in range(BATCH):
                act.wait_ge(turned, b + 1)
                act.copy(o_nat[:, b, :, :].rearrange("p j c -> p (j c)"), bank[b][:]).then_inc(copied, 1)


_INS = ["L0_attn_x", "L0_attn_W_rvk", "L0_attn_W_out", "L0_attn_time_decay", "L0_attn_time_first",
        "L0_ffn_Wqkv", "L0_ffn_q_scale", "L0_ffn_k_scale", "L0_ffn_Wo", "L0_ffn_ln_g", "L0_ffn_ln_b",
        "L0_ffn_W1", "L0_ffn_b1", "L0_ffn_W2", "L0_ffn_b2"]


def kernel(**inputs):
    import numpy as _np
    import concourse.bacc as _bacc
    from concourse import mybir as _mybir
    from concourse.bass_utils import run_bass_kernel_spmd as _run

    nc = _bacc.Bacc("TRN2", target_bir_lowering=False, num_devices=1)
    arrays, args = {}, []
    for name in _INS:
        arrays[f"in_{name}"] = _np.ascontiguousarray(inputs[name])
    for name, a in shape_constants().items():
        arrays[f"const_{name}"] = a
    for name, a in arrays.items():
        args.append(nc.dram_tensor(name, a.shape, _mybir.dt.from_np(a.dtype), kind="ExternalInput").ap())
    args.append(nc.dram_tensor("out_0", (BATCH, SEQ, P), F32, kind="ExternalOutput").ap())
    build(nc, *args)
    r = _run(nc, [arrays], core_ids=[0])
    return r.results[0]["out_0"]
```

```python
from contextlib import ExitStack

import numpy as np

import concourse.bass as bass
from concourse import mybir

F32 = mybir.dt.float32
F32R = mybir.dt.float32r
BF16 = mybir.dt.bfloat16
I32 = mybir.dt.int32
ALU = mybir.AluOpType
ACT = mybir.ActivationFunctionType
AX = mybir.AxisListType

P = 128
BATCH, SEQ = 4, 512
DEPTH, HEADS, DH, WINDOW = 6, 16, 64, 32
INNER = HEADS * DH
NBLK = SEQ // P
NWIN = P // WINDOW
ITEMS = DEPTH * BATCH
BLOCKS = ITEMS * NBLK
CHUNK = 512
HPC = CHUNK // DH
QK_CHUNKS = 2 * INNER // CHUNK
W_CHUNKS = 3 * INNER // CHUNK
CHUNKS = W_CHUNKS
PAIRS = HEADS // 2
DIM_INNER = int(P * 4 * 2 / 3)
HID = [P, P, DIM_INNER - 2 * P]
NHID = len(HID)
QK_SCALE = 8.0
EPS = 1e-5
NEG_BIG = -1e38
MASKED = -1e30
DVE_FIRST, DVE_BODY = 70, 92


def shape_constants():
    ident = np.eye(P, dtype=np.float32)
    center = (np.eye(P) - 1.0 / P).astype(np.float32)
    half = np.arange(0, DH, 2, dtype=np.float32)
    inv_freq = (1.0 / np.float32(10000.0) ** (half / np.float32(DH))).astype(np.float32)
    t = np.arange(SEQ, dtype=np.float32)
    freqs = t[:, None] * inv_freq[None, :]
    base = (half + np.float32(0.4 * DH)) / np.float32(1.4 * DH)
    power = (t - SEQ // 2) / np.float32(WINDOW // 2)
    scale = base[None, :].astype(np.float64) ** power[:, None]
    cos, sin = np.cos(freqs.astype(np.float64)), np.sin(freqs.astype(np.float64))
    rot = np.stack([
        np.concatenate([cos * scale, cos * scale], -1),
        np.concatenate([-sin * scale, sin * scale], -1),
        np.concatenate([cos / scale, cos / scale], -1),
        np.concatenate([-sin / scale, sin / scale], -1),
    ])
    rot = np.ascontiguousarray(rot.reshape(4, NBLK, P, DH).transpose(2, 0, 1, 3)).astype(np.float32)
    q = np.arange(P)[:, None] % WINDOW
    j = np.arange(2 * WINDOW)[None, :]
    own = np.where((j >= q) & (j <= q + WINDOW), 0.0, MASKED)
    first = np.where(j < WINDOW, MASKED, own)
    mask = np.stack([
        np.concatenate([first if w == 0 else own for _ in range(2) for w in range(NWIN)], -1),
        np.concatenate([own for _ in range(2) for w in range(NWIN)], -1),
    ]).transpose(1, 0, 2)
    return {"ident": ident, "center": center, "rot": rot,
            "mask": np.ascontiguousarray(mask.astype(np.float32))}


def need(eng, sem, value):
    if isinstance(value, int) and value <= 0:
        return
    eng.wait_ge(sem, value)


ROOT_STEPS = 10


def root_step(eng, n, x, y, tmp):
    if n == 0:
        return eng.tensor_scalar(y.bitcast(I32), x.bitcast(I32), -0.5, float(0x5F3759DF), ALU.mult, ALU.add)
    if n % 3 == 1:
        return eng.tensor_tensor(tmp, x, y, ALU.mult)
    if n % 3 == 2:
        return eng.scalar_tensor_tensor(tmp, tmp, -0.5, y, ALU.mult, ALU.mult)
    return eng.scalar_tensor_tensor(y, tmp, 1.5, y, ALU.add, ALU.mult)


def rsqrt(eng, seq, x, y, tmp, signal):
    for n in range(ROOT_STEPS - 1):
        seq(root_step(eng, n, x, y, tmp))
    root_step(eng, ROOT_STEPS - 1, x, y, tmp).then_inc(signal, 1)


class Chain:

    def __init__(self, eng, sem, base=0):
        self.eng, self.sem, self.count, self.base = eng, sem, 0, base

    def __call__(self, instruction):
        instruction.then_inc(self.sem, 1)
        self.count += 1
        self.eng.wait_ge(self.sem, self.base + self.count)


WEIGHT_ORDER = [4, 0, 1, 5, 2, 3]


def weight_columns(n):
    return slice(WEIGHT_ORDER[n] * CHUNK, (WEIGHT_ORDER[n] + 1) * CHUNK)


class SplitWeights:

    def __init__(self, sb, sem):
        self.raw = sb("w_raw", [P, 2, CHUNK])
        self.hi, self.lo = sb("w_hi", [P, 3 * INNER], F32R), sb("w_lo", [P, 3 * INNER], F32R)
        self.tables = sb("tables", [P, 2, 4, NBLK, DH])
        self.raw_loaded = [sem("raw_loaded0"), sem("raw_loaded1")]
        self.hi_ready, self.raw_used, self.tables_ready = sem("w_hi_ready"), sem("raw_used"), sem("tables_ready")

    def load(self, sp, w_qkv, layer, c):
        need(sp, self.raw_used, W_CHUNKS * layer + c - 1)
        sp.dma_start(self.raw[:, c % 2, :],
                     w_qkv[layer, :, weight_columns(c)]).then_inc(self.raw_loaded[c % 2], 16)

    def arrived(self, pool, layer, c):
        pool.wait_ge(self.raw_loaded[c % 2], 16 * (W_CHUNKS // 2) * layer + 16 * (c // 2 + 1))

    def split(self, pool, layer, c):
        cols = weight_columns(c)
        pool.tensor_scalar(self.hi[:, cols], self.raw[:, c % 2, :], 1.0, 0.0, ALU.mult, ALU.add).then_inc(self.hi_ready, 1)
        pool.wait_ge(self.hi_ready, W_CHUNKS * layer + c + 1)
        pool.tensor_tensor(self.lo[:, cols], self.raw[:, c % 2, :], self.hi[:, cols].bitcast(F32),
                           ALU.subtract).then_inc(self.raw_used, 1)

    def make_tables(self, pool, layer, qk_rows, rot):
        for kind in range(4):
            if isinstance(layer, int):
                dst, row = self.tables[:, layer % 2, kind, :, :], qk_rows[:, layer, kind, :]
            else:
                dst = self.tables[:, bass.ds(layer % 2, 1), kind, :, :].rearrange("p a t d -> p (a t) d")
                row = qk_rows[:, bass.ds(layer % DEPTH, 1), kind, :].rearrange("p a d -> p (a d)")
            pool.tensor_tensor(dst, rot[:, kind, :, :],
                               row.unsqueeze(1).to_broadcast([P, NBLK, DH]), ALU.mult).then_inc(self.tables_ready, 1)


def build(nc, x, w_rvk, w_out, time_decay, time_first, w_qkv, q_scale, k_scale, w_o, ln_g, ln_b,
          w_1, b_1, w_2, b_2, ident_in, center_in, rot_in, mask_in, out):
    x_res_dram = nc.dram_tensor("x_res_scratch", (P, BATCH, SEQ), F32, kind="Internal").ap()
    with ExitStack() as whole:
        def sb(name, shape, dt=F32, ctx=whole):
            return ctx.enter_context(nc.sbuf_tensor(name, shape, dt))

        def sem(name, ctx=whole):
            return ctx.enter_context(nc.semaphore(name))

        bank = [whole.enter_context(nc.psum_tensor(f"bank{i}", [P, 512], F32)) for i in range(8)]

        ident = sb("ident", [P, P])
        center = sb("center", [P, P])
        mean_col = sb("mean_col", [P, 1])
        x_state = sb("x_state", [P, BATCH, SEQ])
        vecs = sb("vecs", [P, 2 * NHID + 3, DEPTH])
        B1_UP, B1_GATE, B2, LN_G, LN_B = 0, NHID, 2 * NHID, 2 * NHID + 1, 2 * NHID + 2
        qk_rows = sb("qk_rows", [P, DEPTH, 4, DH])
        rot = sb("rot", [P, 4, NBLK, DH])
        mask_bf = sb("mask_bf", [P, 2, 512], BF16)
        ident_bf = sb("ident_bf", [P, P], BF16)

        weights = SplitWeights(sb, sem)

        time_mixing(nc, weights, w_qkv, bank, x, w_rvk, w_out, time_decay, time_first, q_scale, k_scale,
                    ln_g, ln_b, b_1, b_2, ident_in, center_in, rot_in, mask_in, ident, center,
                    mean_col, x_state, vecs, qk_rows, rot, mask_bf, ident_bf, x_res_dram)
        transformer(nc, bank, weights, w_qkv, w_o, w_1, w_2, ident, center, mean_col, x_state, vecs,
                    qk_rows, rot, mask_bf, ident_bf, (B1_UP, B1_GATE, B2, LN_G, LN_B))
        finish(nc, bank, ident, x_state, x_res_dram, out)


def time_mixing(nc, weights, w_qkv, bank, x, w_rvk, w_out, time_decay, time_first, q_scale, k_scale,
                ln_g, ln_b, b_1, b_2, ident_in, center_in, rot_in, mask_in, ident, center,
                mean_col, x_state, vecs, qk_rows, rot, mask_bf, ident_bf, x_res_dram):
    N_TABLE_LOADS = 2 + 2 * 3
    N_VEC = DEPTH * (2 * NHID + 3)
    VECTOR_ROUND = BATCH + 1
    with ExitStack() as ctx:
        def sb(name, shape, dt=F32):
            return ctx.enter_context(nc.sbuf_tensor("mix_" + name, shape, dt))

        def sem(name):
            return ctx.enter_context(nc.semaphore(name))

        x_nat = sb("x_nat", [P, BATCH * NBLK, P])
        w_rvk_nat = sb("w_rvk_nat", [P, 3, P])
        w_out_nat = sb("w_out_nat", [P, P])
        w_rvk_t = sb("w_rvk_t", [P, 3, P])
        w_out_t = sb("w_out_t", [P, P])
        decay = sb("decay", [P, 1])
        first = sb("first", [P, 1])
        exp_decay = sb("exp_decay", [P, 1])
        w_neg = sb("w_neg", [P, 1])
        vec_rows = sb("vec_rows", [DEPTH * (2 * NHID + 3), P])
        mask_f = sb("mask_f", [P, 2, 512])
        stats = sb("stats", [P, BATCH * NBLK, 6])
        mv = sb("mv", [P, BATCH * NBLK, 2])
        var, rstd, nt = (sb(name, [P, BATCH * NBLK]) for name in ("var", "rstd", "nt"))
        var2, rstd2, nt2 = (sb(name, [P, NBLK]) for name in ("var2", "rstd2", "nt2"))
        xn = sb("xn", [P, BATCH * NBLK, P])
        xn_t, x_t = sb("xn_t", [P, 2, SEQ]), sb("x_t", [P, BATCH, SEQ])
        k_s, v_s, er = sb("k_s", [P, 2, SEQ]), sb("v_s", [P, 2, SEQ]), sb("er", [P, 2, SEQ])
        pp, aa, bb = (sb(name, [P, 2, SEQ + 1]) for name in ("pp", "aa", "bb"))
        d1, d2, e1, e2, e2v, pk, g1, g2, f1, f2, f1a, f2v, f1b, num, den, rden, rwkv, x_res, xc, xsq = (
            sb(name, [P, 2, SEQ]) for name in (
                "d1", "d2", "e1", "e2", "e2v", "pk", "g1", "g2", "f1", "f2", "f1a", "f2v", "f1b",
                "num", "den", "rden", "rwkv", "x_res", "xc", "xsq"))

        stored = [sem("a_stored0"), sem("a_stored1")]
        (loaded_x, loaded_w, loaded_t, loaded_v, dve_seq, rows_clear, v_turned, v_copied,
         w_t_ready, w_t_evac, exp_dec) = (sem("a_" + s) for s in (
            "loaded_x", "loaded_w", "loaded_t", "loaded_v", "dve_seq", "rows_clear", "v_turned",
            "v_copied", "w_t_ready", "w_t_evac", "exp_dec"))
        (inv_ready, xn_ready, xt_ready, xt_evac, rvk_ready, rvk_evac, pp_ready, d1_ready, d2_ready,
         pk_ready, g1_ready, g2_ready, e_ready, f_ready, b_ready, f2v_ready, f1b_ready, rwkv_ready,
         o_ready, res_ready, cen_ready, cen_evac, st_ready, rs_ready, bc_ready, xl_ready) = (
            sem("a_" + s) for s in (
                "inv_ready", "xn_ready", "xt_ready", "xt_evac", "rvk_ready", "rvk_evac", "pp_ready",
                "d1_ready", "d2_ready", "pk_ready", "g1_ready", "g2_ready", "e_ready", "f_ready", "b_ready",
                "f2v_ready", "f1b_ready", "rwkv_ready", "o_ready", "res_ready", "cen_ready", "cen_evac",
                "st_ready", "rs_ready", "bc_ready", "xl_ready"))

        def rounds():
            for t in range(BATCH + 2):
                yield tuple(b if 0 <= b < BATCH else None for b in (t, t - 1, t - 2))

        block = ctx.enter_context(nc.Block())

        @block.sync
        def _(sp):
            sp.dma_start(ident[:], ident_in).then_inc(loaded_x, 16)
            sp.dma_start(x_nat[:], x.rearrange("b (j p) c -> p (b j) c", p=P)).then_inc(loaded_x, 16)
            sp.dma_start(w_rvk_nat[:], w_rvk.rearrange("(j p) c -> p j c", p=P)).then_inc(loaded_w, 16)
            sp.dma_start(w_out_nat[:], w_out).then_inc(loaded_w, 16)
            sp.dma_start(center[:], center_in).then_inc(loaded_w, 16)
            sp.dma_start(decay[:], time_decay.rearrange("(p a) -> p a", a=1)).then_inc(loaded_w, 16)
            sp.dma_start(first[:], time_first.rearrange("(p a) -> p a", a=1)).then_inc(loaded_w, 16)
            sp.dma_start(mask_f[:], mask_in).then_inc(loaded_t, 16)
            sp.dma_start(rot[:], rot_in).then_inc(loaded_t, 16)
            h = DH // 2
            for kind, src in ((0, q_scale), (2, k_scale)):
                rows = qk_rows[:, :, kind, :]
                swap = qk_rows[:, :, kind + 1, :]
                for dst, s in ((rows, src), (swap[:, :, 0:h], src[:, h:DH]), (swap[:, :, h:DH], src[:, 0:h])):
                    sp.dma_start(dst, s.rearrange("(o l) d -> o l d", o=1).to_broadcast(
                        [P, DEPTH, s.shape[1]])).then_inc(loaded_t, 16)
            sp.wait_ge(rows_clear, 1)
            for c in range(4):
                weights.load(sp, w_qkv, 0, c)
            for c, src in ((2 * NHID, b_2), (2 * NHID + 1, ln_g), (2 * NHID + 2, ln_b)):
                sp.dma_start(vec_rows[DEPTH * c:DEPTH * (c + 1), :], src).then_inc(loaded_v, 16)
            for part in range(2):
                for j in range(NHID):
                    lo, c = part * DIM_INNER + j * P, part * NHID + j
                    sp.dma_start(vec_rows[DEPTH * c:DEPTH * (c + 1), 0:HID[j]],
                                 b_1[:, lo:lo + HID[j]]).then_inc(loaded_v, 16)
            for b in range(BATCH):
                sp.wait_ge(res_ready, b + 1)
                sp.dma_start(x_res_dram[:, b, :], x_res[:, b % 2, :]).then_inc(stored[b % 2], 16)
                if b == 0:
                    for c in range(4, W_CHUNKS):
                        weights.load(sp, w_qkv, 0, c)
            for done in stored:
                sp.wait_ge(done, 16 * BATCH // 2)

        @block.gpsimd
        def _(pool):
            pool.wait_ge(loaded_t, 16 * N_TABLE_LOADS)
            weights.arrived(pool, 0, 0)
            weights.make_tables(pool, 0, qk_rows, rot)
            for _, b, _ in rounds():
                for c in {None: (), 0: (0, 1), 1: (2, 3), 2: (4, 5), 3: ()}[b]:
                    weights.arrived(pool, 0, c)
                    weights.split(pool, 0, c)
                if b is None:
                    continue
                p = b % 2
                pool.wait_ge(pp_ready, b + 1)
                need(pool, e_ready, 2 * b - 2)
                pool.tensor_tensor(d2[:, p], k_s[:, p], pp[:, p, 1:], ALU.subtract).then_inc(d2_ready, 1)
                pool.wait_ge(pk_ready, b + 1)
                need(pool, f_ready, 2 * b - 2)
                pool.tensor_tensor(g1[:, p], pp[:, p, 0:SEQ], pk[:, p], ALU.subtract).then_inc(g1_ready, 1)
                pool.wait_ge(f_ready, 2 * b + 2)
                need(pool, rwkv_ready, b - 1)
                pool.tensor_tensor(f2v[:, p], f2[:, p], v_s[:, p], ALU.mult).then_inc(f2v_ready, 1)
                pool.wait_ge(b_ready, b + 1)
                pool.tensor_tensor(f1b[:, p], f1[:, p], bb[:, p, 0:SEQ], ALU.mult).then_inc(f1b_ready, 1)

        @block.vector
        def _(dve):
            seq = Chain(dve, dve_seq)
            dve.memset(vec_rows[:], 0.0).then_inc(rows_clear, 1)
            seq(dve.memset(mean_col[:], 1.0 / P))
            for state, start in ((pp, NEG_BIG), (aa, 0.0), (bb, 0.0)):
                seq(dve.memset(state[:, :, 0:1], start))
            dve.wait_ge(exp_dec, 1)
            seq(dve.tensor_scalar(w_neg[:], exp_decay[:], -1.0, None, ALU.mult))
            dve.wait_ge(loaded_x, 32)
            seq(dve.tensor_copy(ident_bf[:], ident[:]))
            for j in range(BATCH * NBLK):
                dve.bn_stats(stats[:, j, :], x_nat[:, j, :]).then_inc(dve_seq, 1)
            seq.count += BATCH * NBLK
            dve.wait_ge(dve_seq, seq.count)
            for j in range(BATCH * NBLK):
                dve.bn_aggr(mv[:, j, :], stats[:, j, :]).then_inc(dve_seq, 1)
            seq.count += BATCH * NBLK
            dve.wait_ge(dve_seq, seq.count)
            seq(dve.tensor_scalar(var[:], mv[:, :, 1], EPS, None, ALU.add))
            rsqrt(dve, seq, var[:], rstd[:], nt[:], inv_ready)
            dve.wait_ge(inv_ready, 1)
            for at, (new, mid, old) in enumerate(rounds()):
                if old is not None:
                    b, p = old, old % 2
                    dve.wait_ge(o_ready, b + 1)
                    need(dve, stored[p], 16 * (b // 2))
                    need(dve, cen_ready, b - 1)
                    dve.tensor_tensor(x_res[:, p], bank[5][:], x_t[:, b], ALU.add).then_inc(res_ready, 1)
                if new is not None:
                    b = new
                    for j in range(b * NBLK, (b + 1) * NBLK):
                        dve.tensor_scalar(xn[:, j, :], x_nat[:, j, :], mv[:, j, 0:1],
                                          rstd[:, j:j + 1], ALU.subtract, ALU.mult).then_inc(xn_ready, 1)
                if mid is not None:
                    b, p = mid, mid % 2
                    dve.wait_ge(rvk_evac, 3 * b + 3)
                    need(dve, g1_ready, b - 1)
                    dve.tensor_tensor_scan(pp[:, p, 1:], w_neg[:].to_broadcast([P, SEQ]), k_s[:, p],
                                           NEG_BIG, ALU.add, ALU.max).then_inc(pp_ready, 1)
                    dve.wait_ge(pp_ready, b + 1)
                    prev = pp[:, p, 0:SEQ]
                    need(dve, e_ready, 2 * (b - 1))
                    dve.scalar_tensor_tensor(d1[:, p], prev, w_neg[:], pp[:, p, 1:], ALU.add,
                                             ALU.subtract).then_inc(d1_ready, 1)
                    dve.scalar_tensor_tensor(pk[:, p], k_s[:, p], first[:], prev, ALU.add,
                                             ALU.max).then_inc(pk_ready, 1)
                    dve.wait_ge(pk_ready, b + 1)
                    need(dve, f_ready, 2 * (b - 1))
                    dve.scalar_tensor_tensor(g2[:, p], k_s[:, p], first[:], pk[:, p], ALU.add,
                                             ALU.subtract).then_inc(g2_ready, 1)
                if old is not None:
                    b, p = old, old % 2
                    dve.wait_ge(st_ready, b + 1)
                    seq(dve.tensor_scalar(var2[:], bank[7][:, 0:NBLK], EPS, None, ALU.add))
                    need(dve, bc_ready, b)
                    rsqrt(dve, seq, var2[:], rstd2[:], nt2[:], rs_ready)
                if mid is not None:
                    b, p = mid, mid % 2
                    dve.wait_ge(e_ready, 2 * b + 2)
                    need(dve, f1b_ready, b - 1)
                    seq(dve.tensor_tensor(e2v[:, p], e2[:, p], v_s[:, p], ALU.mult))
                    dve.tensor_tensor_scan(bb[:, p, 1:], e1[:, p], e2[:, p], 0.0, ALU.mult,
                                           ALU.add).then_inc(b_ready, 1)
                    seq(dve.tensor_tensor_scan(aa[:, p, 1:], e1[:, p], e2v[:, p], 0.0, ALU.mult, ALU.add))
                    dve.wait_ge(f_ready, 2 * b + 2)
                    seq(dve.tensor_tensor(f1a[:, p], f1[:, p], aa[:, p, 0:SEQ], ALU.mult))
                    dve.wait_ge(f2v_ready, b + 1)
                    dve.tensor_tensor(num[:, p], f1a[:, p], f2v[:, p], ALU.add).then_inc(dve_seq, 1)
                    seq.count += 1
                    dve.wait_ge(f1b_ready, b + 1)
                    seq(dve.tensor_tensor(den[:, p], f1b[:, p], f2[:, p], ALU.add))
                    seq(dve.scalar_tensor_tensor(den[:, p], er[:, p], 1.0, den[:, p], ALU.add, ALU.mult))
                    seq(dve.reciprocal(rden[:, p], den[:, p]))
                    need(dve, o_ready, b - 1)
                    dve.tensor_tensor(rwkv[:, p], num[:, p], rden[:, p], ALU.mult).then_inc(rwkv_ready, 1)
                if old is not None:
                    b, p = old, old % 2
                    dve.wait_ge(bc_ready, b + 1)
                    dve.wait_ge(cen_evac, 2 * b + 2)
                    dve.tensor_tensor(x_state[:, b, :], bank[5][:], xc[:, p], ALU.mult).then_inc(xl_ready, 1)
                if at == 1:
                    dve.wait_ge(loaded_t, 16 * N_TABLE_LOADS)
                    seq(dve.tensor_copy(mask_bf[:], mask_f[:]))
                if at == VECTOR_ROUND:
                    dve.wait_ge(v_turned, 1)
                    dve.tensor_copy(vecs[:].rearrange("p c l -> p (c l)"), bank[1][:, 0:N_VEC]).then_inc(v_copied, 1)
            dve.wait_ge(v_copied, 1)
            dve.wait_ge(xl_ready, BATCH)

        @block.scalar
        def _(act):
            act.wait_ge(loaded_w, 80)
            act.activation(exp_decay[:], decay[:], ACT.Exp).then_inc(exp_dec, 1)
            act.wait_ge(w_t_ready, 1)
            act.copy(w_rvk_t[:].rearrange("p j c -> p (j c)"), bank[0][:, 0:3 * P]).then_inc(w_t_evac, 1)
            act.copy(w_out_t[:], bank[0][:, 3 * P:4 * P]).then_inc(w_t_evac, 1)
            for new, mid, old in rounds():
                if old is not None:
                    b, p = old, old % 2
                    act.wait_ge(cen_ready, b + 1)
                    need(act, xl_ready, b - 1)
                    act.activation(xsq[:, p], bank[6][:], ACT.Square).then_inc(cen_evac, 1)
                    act.copy(xc[:, p], bank[6][:]).then_inc(cen_evac, 1)
                if new is not None:
                    b, p = new, new % 2
                    act.wait_ge(xt_ready, 2 * b + 1)
                    need(act, rvk_ready, 3 * (b - 1))
                    act.copy(xn_t[:, p], bank[0][:]).then_inc(xt_evac, 1)
                    act.wait_ge(xt_ready, 2 * b + 2)
                    act.copy(x_t[:, b], bank[1][:]).then_inc(xt_evac, 1)
                if mid is not None:
                    b, p = mid, mid % 2
                    need(act, rwkv_ready, b - 1)
                    act.wait_ge(d1_ready, b + 1)
                    act.activation(e1[:, p], d1[:, p], ACT.Exp).then_inc(e_ready, 1)
                    act.wait_ge(d2_ready, b + 1)
                    act.activation(e2[:, p], d2[:, p], ACT.Exp).then_inc(e_ready, 1)
                    act.wait_ge(g1_ready, b + 1)
                    act.activation(f1[:, p], g1[:, p], ACT.Exp).then_inc(f_ready, 1)
                    act.wait_ge(g2_ready, b + 1)
                    act.activation(f2[:, p], g2[:, p], ACT.Exp).then_inc(f_ready, 1)
                if new is not None:
                    b, p = new, new % 2
                    act.wait_ge(rvk_ready, 3 * b + 3)
                    need(act, rwkv_ready, b - 1)
                    act.activation(er[:, p], bank[2][:], ACT.Exp, scale=-1.0).then_inc(rvk_evac, 1)
                    act.copy(v_s[:, p], bank[3][:]).then_inc(rvk_evac, 1)
                    act.copy(k_s[:, p], bank[4][:]).then_inc(rvk_evac, 1)

        @block.tensor
        def _(pe):
            pe.wait_ge(loaded_x, 32)
            pe.wait_ge(loaded_w, 80)
            for j in range(3):
                pe.transpose(bank[0][:, j * P:(j + 1) * P], w_rvk_nat[:, j, :], ident[:])
            pe.transpose(bank[0][:, 3 * P:4 * P], w_out_nat[:], ident[:]).then_inc(w_t_ready, 1)
            pe.wait_ge(w_t_evac, 2)
            for at, (new, mid, old) in enumerate(rounds()):
                if at == VECTOR_ROUND:
                    pe.wait_ge(xt_evac, 2 * BATCH)
                    pe.wait_ge(loaded_v, 16 * (3 + 2 * NHID))
                    pe.transpose(bank[1][:, 0:N_VEC], vec_rows[:], ident[0:N_VEC, 0:N_VEC]).then_inc(v_turned, 1)
                if old is not None:
                    b, p = old, old % 2
                    pe.wait_ge(rwkv_ready, b + 1)
                    need(pe, xl_ready, b)
                    pe.matmul(bank[5][:], w_out_t[:], rwkv[:, p], start=True, stop=True).then_inc(o_ready, 1)
                    pe.wait_ge(res_ready, b + 1)
                    need(pe, cen_evac, 2 * b)
                    pe.matmul(bank[6][:], center[:], x_res[:, p], start=True, stop=True).then_inc(cen_ready, 1)
                    pe.wait_ge(cen_evac, 2 * b + 1)
                    need(pe, rs_ready, b)
                    for j in range(NBLK):
                        mm = pe.matmul(bank[7][:, j:j + 1], xsq[:, p, j * P:(j + 1) * P], mean_col[:],
                                       start=True, stop=True)
                    mm.then_inc(st_ready, 1)
                if new is not None:
                    b, p = new, new % 2
                    need(pe, xt_evac, 2 * b)
                    pe.wait_ge(xn_ready, 4 * b + 4)
                    for j in range(NBLK):
                        mm = pe.transpose(bank[0][:, j * P:(j + 1) * P], xn[:, b * NBLK + j, :], ident[:])
                    mm.then_inc(xt_ready, 1)
                    for j in range(NBLK):
                        mm = pe.transpose(bank[1][:, j * P:(j + 1) * P], x_nat[:, b * NBLK + j, :], ident[:])
                    mm.then_inc(xt_ready, 1)
                    pe.wait_ge(xt_evac, 2 * b + 1)
                    need(pe, rvk_evac, 3 * b)
                    for j in range(3):
                        pe.matmul(bank[2 + j][:], w_rvk_t[:, j, :], xn_t[:, p], start=True,
                                  stop=True).then_inc(rvk_ready, 1)
                if old is not None:
                    b = old
                    pe.wait_ge(rs_ready, b + 1)
                    for j in range(NBLK):
                        mm = pe.matmul(bank[5][:, j * P:(j + 1) * P],
                                       rstd2[:, j:j + 1].to_broadcast([P, P]), ident[:], start=True, stop=True)
                    mm.then_inc(bc_ready, 1)


def transformer(nc, bank, weights, w_qkv, w_o, w_1, w_2, ident, center, mean_col, x_state, vecs, qk_rows,
                rot, mask_bf, ident_bf, vec_at):
    B1_UP, B1_GATE, B2, LN_G, LN_B = vec_at
    SLOTS, SLOT_OF, V_SLOTS = 8, [1, 2, 4, 5], {0: 0, 3: 1}
    PAD = WINDOW
    NVEC = 2 * NHID + 3
    VAR_AT = 512 - NBLK
    N_CONST = 5
    with ExitStack() as ctx:
        def sb(name, shape, dt=F32):
            return ctx.enter_context(nc.sbuf_tensor(name, shape, dt))

        def sem(name):
            return ctx.enter_context(nc.semaphore(name))

        xs = sb("xs", [P, SEQ])
        xs_hi, xs_lo = sb("xs_hi", [P, SEQ], F32R), sb("xs_lo", [P, SEQ], F32R)
        w_hi, w_lo, tables = weights.hi, weights.lo, weights.tables
        qk = sb("qk", [P, 2, QK_CHUNKS, CHUNK])
        qk_sin = sb("qk_sin", [P, QK_CHUNKS, CHUNK])
        squares = sb("squares", [P, 2, CHUNK])
        norm2 = sb("norm2", [P, QK_CHUNKS * HPC])
        norm_t = sb("norm_t", [P, QK_CHUNKS * HPC])
        rnorm = sb("rnorm", [P, QK_CHUNKS * HPC])
        q_t = sb("q_t", [P, PAIRS, P])
        k_t = sb("k_t", [P, PAIRS, PAD + SEQ])
        v = sb("v", [P, NBLK, 2, HEADS, DH + 1])
        probs = sb("probs", [P, 2, 2, 512])
        row_max = sb("row_max", [P, 2, HPC])
        p_t = sb("p_t", [P, 2, 4, P])
        row_sum = sb("row_sum", [P, 2, 2, 4])
        o = sb("o", [P, 2, 2, 4, DH])
        o_t = sb("o_t", [P, PAIRS, SEQ])
        w_o_s, w_1_s, w_2_s = sb("w_o_s", [P, PAIRS, P]), sb("w_1_s", [P, 2 * DIM_INNER]), sb("w_2_s", [P, NHID, P])
        vec = sb("vec", [P, NVEC])
        x1, xs2 = sb("x1", [P, SEQ]), sb("xs2", [P, SEQ])
        xc, xsq, xn = sb("xc", [P, SEQ]), sb("xsq", [P, SEQ]), sb("xn", [P, SEQ])
        var, rstd = sb("var", [P, NBLK]), sb("rstd", [P, NBLK])
        var_t = sb("var_t", [P, NBLK])
        gated, hidden = sb("gated", [P, SEQ]), sb("hidden", [P, NHID, SEQ])

        tail_w_loaded = sem("tail_w_loaded")
        chunk_ready, qk_turned, scores_ready = sem("chunk_ready"), sem("qk_turned"), sem("scores_ready")
        p_turned, o_ready, o_turned = sem("p_turned"), sem("o_ready"), sem("o_turned")
        wo_ready, cen_ready, var_ready, rstd_wide = (sem(s) for s in ("wo_ready", "cen_ready", "var_ready", "rstd_wide"))
        gate_ready, up_ready, y_ready = sem("gate_ready"), sem("up_ready"), sem("y_ready")
        v_moved = [sem("v_moved0"), sem("v_moved1")]
        xs_copied = sem("xs_copied")
        chunk_free, qk_evac, exp_ready = sem("chunk_free"), sem("qk_evac"), sem("exp_ready")
        p_evac, o_t_evac = sem("p_evac"), sem("o_t_evac")
        cen_evac, gelu_ready = sem("cen_evac"), sem("gelu_ready")
        xs_ready, rotated, summed, rnorm_ready = (sem(s) for s in ("xs_ready", "rotated", "summed", "rnorm_ready"))
        shifted_ready, o_normed, x1_done, xs2_ready = (sem(s) for s in ("scores_shifted", "o_normed", "x1_done", "xs2_ready"))
        rstd_ready, xn_ready, hidden_ready, x2_done = (sem(s) for s in ("rstd_ready", "xn_ready", "hidden_ready", "x2_done"))
        dve_seq, constants_ready = sem("dve_seq"), sem("constants_ready")
        qk_added, qk_normed = sem("qk_added"), sem("qk_normed")
        raw_used, tables_ready = weights.raw_used, weights.tables_ready

        def batch_slot(item):
            if isinstance(item, int):
                return x_state[:, item % BATCH, :]
            return x_state[:, bass.ds(item % BATCH, 1), :].rearrange("p b t -> p (b t)")

        def moved_count(item, t):
            return 48 * item + (16 if t == 0 else 48) if t % 2 == 0 else 64 * item + 32 * (t // 2 + 1)

        def layer_of(item):
            return item // BATCH

        def steps(item, head, tail, back):
            for t in range(NBLK):
                if t - back >= 0:
                    yield (item, t - back, NBLK * item + t - back) if head else None
                else:
                    yield (item - 1, t - back + NBLK, NBLK * item + t - back) if tail else None

        def run(eng, body):
            body(0, True, False)
            with eng.Fori(1, ITEMS) as item:
                body(item, True, True)
            body(ITEMS, False, True)

        block = ctx.enter_context(nc.Block())

        @block.sync
        def _(sp):
            for layer in range(DEPTH):
                if layer > 0:
                    for c in range(W_CHUNKS):
                        weights.load(sp, w_qkv, layer, c)
                need(sp, x2_done, BATCH * layer)
                sp.dma_start(w_o_s[:], w_o[layer].rearrange("(p r) n -> r p n", r=P)).then_inc(tail_w_loaded, 16)
                sp.dma_start(w_1_s[:], w_1[layer]).then_inc(tail_w_loaded, 16)
                sp.dma_start(w_2_s[:, 0:2, :], w_2[layer, 0:2 * P].rearrange("(j r) n -> r j n", r=P)).then_inc(tail_w_loaded, 16)
                sp.dma_start(w_2_s[0:HID[2], 2, :], w_2[layer, 2 * P:]).then_inc(tail_w_loaded, 16)

        @block.gpsimd
        def _(pool):
            def split_tokens(item, part):
                cols = slice(part * SEQ // 2, (part + 1) * SEQ // 2)
                pool.wait_ge(xs_copied, 3 * (2 * item + part + 1))
                pool.tensor_tensor(xs_lo[:, cols], xs[:, cols],
                                   xs_hi[:, cols].bitcast(F32), ALU.subtract).then_inc(xs_ready, 1)

            split_tokens(0, 0)

            def body(item, head, tail):
                past = (item + 1 + 32 - ITEMS) // 32
                layer = (item + 1) % ITEMS // BATCH

                def before_next_layer():
                    return pool.If((item + 1) % BATCH + past == 0)

                for now in steps(item, head, tail, 0):
                    if now is None:
                        continue
                    _, t, g = now
                    par, prepare = t % 2, t == NBLK - 1 and not isinstance(item, int)
                    if t == NBLK - 2 and not isinstance(item, int):
                        with before_next_layer():
                            weights.make_tables(pool, layer, qk_rows, rot)
                    for c in range(QK_CHUNKS):
                        if prepare:
                            weights.arrived(pool, layer, c)
                        pool.wait_ge(rotated, QK_CHUNKS * g + c + 1)
                        pool.tensor_tensor(qk[:, par, c, :], qk[:, par, c, :], qk_sin[:, c, :],
                                           ALU.add).then_inc(qk_added, 1)
                        if t == 0 and c == 3:
                            split_tokens(item, 1)
                        if t == NBLK - 1 and c == 1:
                            split_tokens(item + 1, 0)
                        if prepare:
                            with before_next_layer():
                                weights.split(pool, layer, c)
                    for c in range(QK_CHUNKS):
                        if prepare and c == 1:
                            weights.arrived(pool, layer, 4)
                        if prepare and c == 2:
                            weights.arrived(pool, layer, 5)
                        if c == 0:
                            pool.wait_ge(rnorm_ready, g + 1)
                        pool.wait_ge(qk_added, QK_CHUNKS * g + c + 1)
                        view = qk[:, par, c, :].rearrange("p (h d) -> p h d", d=DH)
                        pool.tensor_tensor(view, view, rnorm[:, c * HPC:(c + 1) * HPC].unsqueeze(2)
                                           .to_broadcast([P, HPC, DH]), ALU.mult).then_inc(qk_normed, 1)
                        if prepare and c in (1, 2):
                            with before_next_layer():
                                weights.split(pool, layer, 3 + c)

            run(pool, body)

        @block.vector
        def _(dve):
            seq = Chain(dve, dve_seq)
            half = P // 2

            for z in (xs[:, 0:1], k_t[:, :, 0:PAD], xs2[:, 0:1], v[0:PAD, 0, 0, :, :]):
                dve.memset(z, 0.0).then_inc(constants_ready, 1)
            dve.memset(v[:, :, 1, :, DH:DH + 1], 1.0).then_inc(constants_ready, 1)
            dve.wait_ge(constants_ready, N_CONST)
            chained = {}

            roots = {}

            def start_roots(now, tail_item):
                if tail_item is not None:
                    dve.wait_ge(var_ready, tail_item + 1)
                    dve.tensor_scalar(var[:], bank[6][:, VAR_AT:VAR_AT + NBLK], EPS, None, ALU.add).then_inc(dve_seq, 1)
                    seq.count += 1
                if now:
                    _, t, g = now
                    dve.wait_ge(summed, QK_CHUNKS * (g + 1))
                    dve.tensor_scalar(norm2[:], norm2[:], 1e-24, None, ALU.max).then_inc(dve_seq, 1)
                    seq.count += 1
                roots["at"] = seq.base + seq.count

            def advance_roots(now, steps, tail_item):
                tiles = []
                if now:
                    _, t, g = now
                    tiles.append((norm2[:], rnorm[:], norm_t[:], rnorm_ready))
                if tail_item is not None:
                    tiles.append((var[:], rstd[:], var_t[:], rstd_ready))
                for n in steps if tiles else ():
                    dve.wait_ge(dve_seq, roots["at"])
                    if n == 0 and now:
                        need(dve, qk_normed, QK_CHUNKS * g)
                    for x, y, tmp, signal in tiles:
                        last = n == ROOT_STEPS - 1
                        root_step(dve, n, x, y, tmp).then_inc(signal if last else dve_seq, 1)
                        seq.count += 0 if last else 1
                    roots["at"] = seq.base + seq.count

            def rotate(now, item, c):
                _, t, g = now

                def table(k):
                    if isinstance(item, int):
                        return tables[:, layer_of(item) % 2, k, t, :]
                    return tables[:, bass.ds(layer_of(item) % 2, 1), k, t, :].rearrange("p a d -> p (a d)")

                kind = 2 * (c // 2)
                dve.wait_ge(chunk_ready, CHUNKS * g + SLOT_OF[c] + 1)
                need(dve, qk_turned, QK_CHUNKS * (g - 2) + c + 1)
                dve.tensor_tensor(qk[:, t % 2, c, :].rearrange("p (h d) -> p h d", d=DH),
                                  bank[SLOT_OF[c] % 2][:].rearrange("p (h d) -> p h d", d=DH),
                                  table(kind).unsqueeze(1).to_broadcast([P, HPC, DH]),
                                  ALU.mult).then_inc(dve_seq, 1)
                seq.count += 1
                need(dve, qk_added, QK_CHUNKS * (g - 1) + c + 1)
                dve.tensor_tensor(
                    qk_sin[:, c, :].rearrange("p (h a d) -> p h a d", a=2, d=DH // 2),
                    bank[SLOT_OF[c] % 2][:].rearrange("p (h a d) -> p h a d", a=2, d=DH // 2)[:, :, ::-1, :],
                    table(kind + 1).rearrange("p (a d) -> p a d", a=2).unsqueeze(1)
                    .to_broadcast([P, HPC, 2, DH // 2]), ALU.mult).then_inc(rotated, 1)

            def sum_squares(now, c):
                _, t, g = now
                dve.wait_ge(chunk_free, CHUNKS * g + SLOT_OF[c] + 1)
                dve.tensor_reduce(norm2[:, c * HPC:(c + 1) * HPC],
                                  squares[:, c % 2, :].rearrange("p (h d) -> p h d", d=DH),
                                  AX.X, ALU.add).then_inc(summed, 1)

            def sums_of(w):
                return bank[6 + w][:, 0:4 * (DH + 1)].rearrange("p (s d) -> p s d", d=DH + 1)

            def invert_sums(now, m, w):
                _, t, g = now
                dve.wait_ge(o_ready, 4 * g + 2 * m + w + 1)
                dve.reciprocal(row_sum[:, m, w, :].unsqueeze(2), sums_of(w)[:, :, DH:DH + 1]).then_inc(dve_seq, 1)
                seq.count += 1
                return seq.base + seq.count

            def normalise(now, m, w, inverted):
                _, t, g = now
                dve.wait_ge(dve_seq, inverted)
                need(dve, o_turned, 2 * (g - 1) + m + 1)
                dve.tensor_tensor(o[:, m, w, :, :], sums_of(w)[:, :, 0:DH],
                                  row_sum[:, m, w, :].unsqueeze(2).to_broadcast([P, 4, DH]),
                                  ALU.mult).then_inc(o_normed, 1)

            def shift_scores(now, r, halfway):
                _, t, g = now
                view = bank[4 + r][:].rearrange("p (s k) -> p s k", k=2 * WINDOW)
                dve.wait_ge(scores_ready, 2 * g + r + 1)
                dve.tensor_reduce(row_max[:, r, :], view, AX.X, ALU.max).then_inc(dve_seq, 1)
                seq.count += 1
                maximum_at = seq.base + seq.count
                halfway()
                dve.wait_ge(dve_seq, maximum_at)
                need(dve, p_turned, 2 * (g - 2) + r + 1)
                dve.tensor_tensor(probs[:, t % 2, r, :].rearrange("p (s k) -> p s k", k=2 * WINDOW),
                                  view, row_max[:, r, :].unsqueeze(2).to_broadcast([P, HPC, 2 * WINDOW]),
                                  ALU.subtract).then_inc(shifted_ready, 1)

            def body(item, head, tail):
                seq.count = 0
                first = isinstance(item, int) and item == 0
                seq.base = 0 if first else DVE_FIRST + (item - 1) * DVE_BODY
                m = item - 1
                for step, (a, b, c) in enumerate(zip(*(steps(item, head, tail, back) for back in range(3)))):
                    ffn = tail and step == NBLK - 1
                    for slot in range(SLOTS):
                        if ffn and 3 <= slot < 3 + NHID:
                            j = slot - 3
                            n = HID[j]
                            dve.wait_ge(gelu_ready, NHID * m + j + 1)
                            dve.wait_ge(up_ready, NHID * m + j + 1)
                            dve.scalar_tensor_tensor(hidden[0:n, j, :], bank[4][0:n, :], vec[0:n, B1_UP + j:B1_UP + j + 1],
                                                     gated[0:n, :], ALU.add, ALU.mult).then_inc(hidden_ready, 1)
                        if tail and step == 2 and slot == 3:
                            if isinstance(m, int):
                                seq(dve.tensor_copy(vec[:], vecs[:, :, layer_of(m)]))
                            else:
                                seq(dve.tensor_copy(vec[:], vecs[:, :, bass.ds(layer_of(m), 1)].rearrange("p c l -> p (c l)")))
                            dve.wait_ge(wo_ready, item)
                            dve.tensor_tensor(x1[:], bank[4][:], batch_slot(m), ALU.add).then_inc(x1_done, 1)
                            dve.wait_ge(x1_done, item)
                            dve.tensor_copy(xs2[half:P, 1:SEQ], x1[half:P, 0:SEQ - 1]).then_inc(xs2_ready, 1)
                        root_tail = m if tail and step == 2 else None
                        if c and 3 <= slot < 7:
                            place = divmod(slot - 3, 2)
                            inverted = invert_sums(c, *place)
                        if a and slot == 1:
                            if step == 0:
                                dve.wait_ge(tables_ready, 4 * (layer_of(item) + 1))
                            rotate(a, item, 0)
                        if a and slot == 2:
                            rotate(a, item, 1)
                            sum_squares(a, 0)
                        if a and slot == 4:
                            rotate(a, item, 2)
                        if a and slot == 5:
                            sum_squares(a, 2)
                        if ffn and slot == 6:
                            dve.wait_ge(y_ready, item)
                            dve.scalar_tensor_tensor(batch_slot(m), bank[5][:], vec[:, B2:B2 + 1], x1[:],
                                                     ALU.add, ALU.add).then_inc(x2_done, 1)
                            dve.wait_ge(x2_done, item)
                        if a and slot == 6:
                            sum_squares(a, 3)
                        if c and 3 <= slot < 7:
                            normalise(c, *place, inverted)
                        if a and slot == 3:
                            sum_squares(a, 1)
                        if a and slot == 5:
                            rotate(a, item, 3)
                        if slot == 6:
                            start_roots(a, root_tail)
                            if b:
                                shift_scores(b, 0, lambda: advance_roots(a, [0], root_tail))
                            else:
                                advance_roots(a, [0], root_tail)
                            advance_roots(a, [1, 2, 3, 4], root_tail)
                        if slot == 7:
                            if b:
                                shift_scores(b, 1, lambda: advance_roots(a, [5], root_tail))
                            else:
                                advance_roots(a, [5], root_tail)
                            advance_roots(a, range(6, ROOT_STEPS), root_tail)
                        if ffn and slot == 1:
                            dve.wait_ge(rstd_wide, item)
                            dve.wait_ge(cen_evac, 2 * item)
                            seq(dve.scalar_tensor_tensor(xn[:], xc[:], vec[:, LN_G:LN_G + 1], bank[4][:],
                                                         ALU.mult, ALU.mult))
                            dve.tensor_scalar(xn[:], xn[:], vec[:, LN_B:LN_B + 1], None, ALU.add).then_inc(xn_ready, 1)
                chained[(head, tail)] = seq.count

            body(0, True, False)
            assert chained[(True, False)] == DVE_FIRST, chained
            with dve.Fori(1, ITEMS) as item:
                body(item, True, True)
            assert chained[(True, True)] == DVE_BODY, chained
            body(ITEMS, False, True)

        @block.scalar
        def _(act):
            half = P // 2

            def shift_tokens(item, part):
                xb = batch_slot(item)
                lo, hi = part * SEQ // 2, (part + 1) * SEQ // 2
                before, lo1 = 3 * (2 * item + part), max(lo, 1)
                need(act, xs_ready, 2 * item + part)
                act.copy(xs[0:half, lo:hi], xb[0:half, lo:hi]).then_inc(xs_copied, 1)
                act.copy(xs[half:P, lo1:hi], xb[half:P, lo1 - 1:hi - 1]).then_inc(xs_copied, 1)
                act.wait_ge(xs_copied, before + 2)
                act.copy(xs_hi[:, lo:hi], xs[:, lo:hi]).then_inc(xs_copied, 1)

            act.wait_ge(constants_ready, N_CONST)
            shift_tokens(0, 0)

            def square(now, n):
                _, t, g = now
                act.wait_ge(rotated, QK_CHUNKS * g + n + 1)
                need(act, summed, QK_CHUNKS * g + n - 1)
                act.activation(squares[:, n % 2, :], bank[SLOT_OF[n] % 2][:], ACT.Square).then_inc(chunk_free, 1)

            def take_v(now, slot):
                item, t, g = now
                heads = slice(V_SLOTS[slot] * HPC, (V_SLOTS[slot] + 1) * HPC)
                act.wait_ge(chunk_ready, CHUNKS * g + slot + 1)
                if slot == 0 and not (isinstance(item, int) and item == 0):
                    act.wait_ge(o_ready, 4 * (g - NBLK) + 4)
                    for tt in (t, min(t + 1, NBLK - 1)):
                        act.wait_ge(v_moved[tt % 2], moved_count(item - 1, tt))
                act.copy(v[:, t, 1, heads, 0:DH],
                         bank[slot % 2][:].rearrange("p (h d) -> p h d", d=DH)).then_inc(chunk_free, 1)

            def move_v(now):
                item, t, g = now
                if t >= 2:
                    act.wait_ge(v_moved[t % 2], moved_count(item, t - 2))
                elif not (isinstance(item, int) and item == 0):
                    act.wait_ge(v_moved[t % 2], moved_count(item - 1, t + 2))
                act.wait_ge(chunk_free, CHUNKS * g + 4)
                act.dma_start(v[PAD:P, t, 0, :, :], v[0:P - PAD, t, 1, :, :]).then_inc(v_moved[t % 2], 16)
                if t > 0:
                    act.dma_start(v[0:PAD, t, 0, :, :], v[P - PAD:P, t - 1, 1, :, :]).then_inc(v_moved[t % 2], 16)

            def take_qk(now, n):
                _, t, g = now
                act.wait_ge(qk_turned, QK_CHUNKS * g + n + 1)
                need(act, scores_ready, 2 * g)
                pairs = slice(4 * (n % 2), 4 * (n % 2) + 4)
                dst = q_t[:, pairs, :] if n < 2 else k_t[:, pairs, PAD + P * t:PAD + P * (t + 1)]
                act.copy(dst, bank[2 + n % 2][:].rearrange("p (h d) -> p h d", d=P)).then_inc(qk_evac, 1)

            def exponentiate(now, r):
                _, t, g = now
                act.wait_ge(shifted_ready, 2 * g + r + 1)
                act.activation(probs[:, t % 2, r, :], probs[:, t % 2, r, :], ACT.Exp,
                               scale=QK_SCALE).then_inc(exp_ready, 1)

            def take_probs(now, r):
                _, t, g = now
                act.wait_ge(p_turned, 2 * g + r + 1)
                need(act, o_ready, 4 * g)
                act.copy(p_t[:, r, :, :], bank[2 + r][:].rearrange("p (s q) -> p s q", q=P)).then_inc(p_evac, 1)

            def take_o(now, n, item):
                _, t, g = now
                act.wait_ge(o_turned, 2 * g + n + 1)
                if t == 0 and n == 0:
                    need(act, wo_ready, item)
                dst = o_t[:, :, P * t:P * (t + 1)].rearrange("p a (w m q) -> p w m a q", w=2, q=WINDOW)
                act.copy(dst[:, :, n, :, :],
                         bank[2 + n][:].rearrange("p (w a q) -> p w a q", w=2, q=WINDOW)).then_inc(o_t_evac, 1)

            def body(item, head, tail):
                m = item - 1
                for step, (a, b, c) in enumerate(zip(*(steps(item, head, tail, back) for back in range(3)))):
                    for slot in range(SLOTS):
                        if a and slot == 1 and step == NBLK - 1:
                            act.wait_ge(chunk_ready, CHUNKS * (NBLK * item + NBLK - 1))
                            shift_tokens(item + 1, 0)
                        if a and slot == 4 and step == 0:
                            shift_tokens(item, 1)
                        if tail and step == NBLK - 1 and 3 <= slot < 3 + NHID:
                            j = slot - 3
                            n = HID[j]
                            act.wait_ge(gate_ready, NHID * m + j + 1)
                            if j > 0:
                                act.wait_ge(hidden_ready, NHID * m + j)
                            act.activation(gated[0:n, :], bank[5][0:n, :], ACT.Gelu,
                                           bias=vec[0:n, B1_GATE + j:B1_GATE + j + 1]).then_inc(gelu_ready, 1)
                        if a and slot == 0:
                            take_v(a, 0)
                        if c and slot == 0:
                            take_probs(c, 0)
                        if a and slot - 1 in SLOT_OF:
                            square(a, SLOT_OF.index(slot - 1))
                        if c and slot == 1:
                            take_probs(c, 1)
                        if tail and step == 2 and slot == 4:
                            act.wait_ge(x1_done, item)
                            act.copy(xs2[0:half, :], x1[0:half, :]).then_inc(xs2_ready, 1)
                        if tail and step == 2 and slot == 5:
                            act.wait_ge(cen_ready, item)
                            act.activation(xsq[:], bank[5][:], ACT.Square).then_inc(cen_evac, 1)
                            act.copy(xc[:], bank[5][:]).then_inc(cen_evac, 1)
                        if b and 2 <= slot < 6:
                            take_qk(b, slot - 2)
                        if b and slot == 7:
                            exponentiate(b, 0)
                        if a and slot == 3:
                            take_v(a, slot)
                        if a and slot == 6:
                            move_v(a)
                        if c and slot >= 6:
                            take_o(c, slot - 6, item)
                        if b and slot == 7:
                            exponentiate(b, 1)

            run(act, body)

        @block.tensor
        def _(pe):
            def project(now, item, slot):
                _, t, g = now
                wc = QK_CHUNKS + V_SLOTS[slot] if slot in V_SLOTS else SLOT_OF.index(slot)
                if t == 0:
                    pe.wait_ge(raw_used, W_CHUNKS * layer_of(item) + WEIGHT_ORDER.index(wc) + 1)
                if t % 2 == 0 and slot == 0:
                    pe.wait_ge(xs_ready, 2 * item + t // 2 + 1)
                    if isinstance(item, int):
                        pe.wait_ge(constants_ready, N_CONST)
                need(pe, chunk_free, CHUNKS * g + slot - 1)
                l_hi, l_lo = xs_hi[:, P * t:P * (t + 1)], xs_lo[:, P * t:P * (t + 1)]
                cols = slice(wc * CHUNK, (wc + 1) * CHUNK)
                pe.matmul(bank[slot % 2][:], l_hi, w_hi[:, cols], start=True, stop=False)
                pe.matmul(bank[slot % 2][:], l_hi, w_lo[:, cols], start=False, stop=False)
                pe.matmul(bank[slot % 2][:], l_lo, w_hi[:, cols], start=False, stop=True).then_inc(chunk_ready, 1)

            def turn_qk(now, c, weighed):
                _, t, g = now
                pe.wait_ge(qk_normed, QK_CHUNKS * g + c + 1)
                if c < 2:
                    need(pe, p_evac, 2 * (g - 1) + c + 1)
                else:
                    pe.wait_ge(qk_evac, QK_CHUNKS * g + c - 1)
                for j in range(4):
                    if j == 3 and weighed:
                        before_weigh(weighed, *divmod(c, 2))
                    mm = pe.transpose(bank[2 + c % 2][:, j * P:(j + 1) * P],
                                      qk[:, t % 2, c, j * P:(j + 1) * P], ident[:])
                mm.then_inc(qk_turned, 1)

            def turn_probs(now, r):
                _, t, g = now
                pe.wait_ge(exp_ready, 2 * g + r + 1)
                need(pe, o_t_evac, 2 * g - 1 + r)
                for j in range(4):
                    mm = pe.transpose(bank[2 + r][:, j * P:(j + 1) * P],
                                      probs[:, t % 2, r, j * P:(j + 1) * P], ident[:])
                mm.then_inc(p_turned, 1)

            def turn_o(now, m, beside_b):
                _, t, g = now
                pe.wait_ge(o_normed, 4 * g + 2 * m + 2)
                if beside_b:
                    pe.wait_ge(qk_evac, QK_CHUNKS * (g + 1) + m + 3)
                for w in range(2):
                    for s in range(2):
                        mm = pe.transpose(bank[2 + m][:, (2 * w + s) * P:(2 * w + s + 1) * P],
                                          o[:, m, w, 2 * s:2 * s + 2, :].rearrange("p r d -> p (r d)"), ident[:])
                mm.then_inc(o_turned, 1)

            def score(now, r):
                _, t, g = now
                pe.wait_ge(qk_evac, QK_CHUNKS * (g + 1))
                need(pe, shifted_ready, 2 * g + r - 1)
                s_bank = bank[4 + r]
                pe.matmul(s_bank[:], ident_bf[:], mask_bf[:, min(t, 1), :], start=True, stop=True)
                for s in range(2):
                    for place in range(NWIN):
                        w = 2 * (place % 2) + place // 2
                        for h in range(4):
                            pair = 4 * s + h
                            row = slice(DH * r, DH * (r + 1))
                            col = (NWIN * s + place) * 2 * WINDOW
                            mm = pe.matmul(s_bank[WINDOW * h:WINDOW * (h + 1), col:col + 2 * WINDOW],
                                           q_t[row, pair, WINDOW * w:WINDOW * (w + 1)],
                                           k_t[row, pair, P * t + WINDOW * w:P * t + WINDOW * w + 2 * WINDOW],
                                           start=False, stop=True, skip_group_check=True)
                mm.then_inc(scores_ready, 1)

            def before_weigh(now, m, w):
                _, t, g = now
                pe.wait_ge(p_evac, 2 * (g + 1))
                need(pe, o_normed, 4 * g + 2 * m + w - 1)
                if m == w == 0:
                    pe.wait_ge(v_moved[t % 2], moved_count(g // NBLK, t))

            def weigh(now, m, w):
                _, t, g = now
                row = slice(2 * WINDOW * w, 2 * WINDOW * (w + 1))
                for s in range(2):
                    for r in range(2):
                        for h in range(4):
                            quad = 2 * s + r
                            mm = pe.matmul(bank[6 + w][WINDOW * h:WINDOW * (h + 1), quad * (DH + 1):(quad + 1) * (DH + 1)],
                                           p_t[row, r, 2 * s + m, WINDOW * h:WINDOW * (h + 1)],
                                           v[row, t, m, 8 * s + 2 * h + r, :], start=True, stop=True)
                mm.then_inc(o_ready, 1)

            def tail_product(item, step, slot, scored):
                m = item - 1
                if step == 2 and slot in (1, 2):
                    if slot == 1:
                        pe.wait_ge(tail_w_loaded, 64 * (layer_of(m) + 1))
                        pe.wait_ge(o_t_evac, 2 * NBLK * item)
                        pe.wait_ge(shifted_ready, scored - 1)
                    half = PAIRS // 2
                    for p in range((slot - 1) * half, slot * half):
                        mm = pe.matmul(bank[4][:], w_o_s[:, p, :], o_t[:, p, :], start=(p == 0), stop=(p == PAIRS - 1))
                    if slot == 2:
                        mm.then_inc(wo_ready, 1)
                if step == 2 and slot == 4:
                    pe.wait_ge(xs2_ready, 2 * item)
                    pe.wait_ge(shifted_ready, scored)
                    pe.matmul(bank[5][:], center[:], xs2[:], start=True, stop=True).then_inc(cen_ready, 1)
                if step == 3 and slot == 1:
                    pe.wait_ge(rstd_ready, item)
                    pe.wait_ge(shifted_ready, scored - 1)
                    for j in range(NBLK):
                        mm = pe.matmul(bank[4][:, j * P:(j + 1) * P], rstd[:, j:j + 1].to_broadcast([P, P]), ident[:],
                                       start=True, stop=True)
                    mm.then_inc(rstd_wide, 1)
                if step == 3 and 2 <= slot < 2 + NHID:
                    j = slot - 2
                    n = HID[j]
                    if j == 0:
                        pe.wait_ge(xn_ready, item)
                        pe.wait_ge(shifted_ready, scored)
                    else:
                        pe.wait_ge(hidden_ready, NHID * m + j)
                    gate = DIM_INNER + j * P
                    pe.matmul(bank[5][0:n, :], w_1_s[:, gate:gate + n], xn[:], start=True, stop=True).then_inc(gate_ready, 1)
                    pe.matmul(bank[4][0:n, :], w_1_s[:, j * P:j * P + n], xn[:], start=True, stop=True).then_inc(up_ready, 1)
                if step == 3 and slot == 5:
                    pe.wait_ge(hidden_ready, NHID * item)
                    for j in range(NHID):
                        n = HID[j]
                        mm = pe.matmul(bank[5][:], w_2_s[0:n, j, :], hidden[0:n, j, :], start=(j == 0), stop=(j == NHID - 1))
                    mm.then_inc(y_ready, 1)

            def body(item, head, tail):
                for step, (a, b, c) in enumerate(zip(*(steps(item, head, tail, back) for back in range(3)))):
                    scored = 2 * (NBLK * item + step - 1) if head else 2 * NBLK * item
                    weighed = NBLK * item + step - 1 if head else NBLK * item
                    for slot in range(SLOTS):
                        if tail and step == 2 and slot == 6:
                            pe.wait_ge(cen_evac, 2 * item)
                            pe.wait_ge(o_normed, 4 * weighed - 1)
                            for j in range(NBLK):
                                mm = pe.matmul(bank[6][:, VAR_AT + j:VAR_AT + j + 1], xsq[:, j * P:(j + 1) * P],
                                               mean_col[:], start=True, stop=True)
                            mm.then_inc(var_ready, 1)
                        if b and slot >= 6:
                            if tail and step == 2 and slot == 6:
                                pe.wait_ge(x1_done, item)
                            if tail and step == 2 and slot == 7:
                                pe.wait_ge(cen_evac, 2 * item)
                            if tail and step == 3 and slot == 7:
                                pe.wait_ge(x2_done, item)
                            score(b, slot - 6)
                        if a and slot < CHUNKS:
                            project(a, item, slot)
                        if c and slot < 2:
                            turn_probs(c, slot)
                        if b and 2 <= slot < 6:
                            turn_qk(b, slot - 2, c)
                        elif c and 2 <= slot < 6:
                            before_weigh(c, *divmod(slot - 2, 2))
                        if c and slot == 6:
                            turn_o(c, 0, b)
                        if c and slot == 7:
                            turn_o(c, 1, b)
                        if c and 2 <= slot < 6:
                            weigh(c, *divmod(slot - 2, 2))
                        if tail:
                            tail_product(item, step, slot, scored)

            run(pe, body)



def finish(nc, bank, ident, x_state, x_res_dram, out):
    with ExitStack() as ctx:
        x_res = ctx.enter_context(nc.sbuf_tensor("f_x_res", [P, BATCH, SEQ], F32))
        total = ctx.enter_context(nc.sbuf_tensor("f_total", [P, BATCH, SEQ], F32))
        o_nat = ctx.enter_context(nc.sbuf_tensor("f_o_nat", [P, BATCH, NBLK, P], F32))
        loaded, added, turned, copied, stored = (ctx.enter_context(nc.semaphore(s)) for s in (
            "f_loaded", "f_added", "f_turned", "f_copied", "f_stored"))
        block = ctx.enter_context(nc.Block())

        @block.sync
        def _(sp):
            for b in range(BATCH):
                sp.dma_start(x_res[:, b, :], x_res_dram[:, b, :]).then_inc(loaded, 16)
            for b in range(BATCH):
                sp.wait_ge(copied, b + 1)
                sp.dma_start(out[b].rearrange("(j p) c -> p j c", p=P), o_nat[:, b, :, :]).then_inc(stored, 16)
            sp.wait_ge(stored, 16 * BATCH)

        @block.vector
        def _(dve):
            dve.wait_ge(loaded, 16 * BATCH)
            for b in range(BATCH):
                dve.tensor_tensor(total[:, b, :], x_res[:, b, :], x_state[:, b, :], ALU.add).then_inc(added, 1)

        @block.tensor
        def _(pe):
            for b in range(BATCH):
                pe.wait_ge(added, b + 1)
                for j in range(NBLK):
                    mm = pe.transpose(bank[b][:, j * P:(j + 1) * P], total[:, b, j * P:(j + 1) * P], ident[:])
                mm.then_inc(turned, 1)

        @block.scalar
        def _(act):
            for b in range(BATCH):
                act.wait_ge(turned, b + 1)
                act.copy(o_nat[:, b, :, :].rearrange("p j c -> p (j c)"), bank[b][:]).then_inc(copied, 1)


_INS = ["L0_attn_x", "L0_attn_W_rvk", "L0_attn_W_out", "L0_attn_time_decay", "L0_attn_time_first",
        "L0_ffn_Wqkv", "L0_ffn_q_scale", "L0_ffn_k_scale", "L0_ffn_Wo", "L0_ffn_ln_g", "L0_ffn_ln_b",
        "L0_ffn_W1", "L0_ffn_b1", "L0_ffn_W2", "L0_ffn_b2"]


def kernel(**inputs):
    import numpy as _np
    import concourse.bacc as _bacc
    from concourse import mybir as _mybir
    from concourse.bass_utils import run_bass_kernel_spmd as _run

    nc = _bacc.Bacc("TRN2", target_bir_lowering=False, num_devices=1)
    arrays, args = {}, []
    for name in _INS:
        arrays[f"in_{name}"] = _np.ascontiguousarray(inputs[name])
    for name, a in shape_constants().items():
        arrays[f"const_{name}"] = a
    for name, a in arrays.items():
        args.append(nc.dram_tensor(name, a.shape, _mybir.dt.from_np(a.dtype), kind="ExternalInput").ap())
    args.append(nc.dram_tensor("out_0", (BATCH, SEQ, P), F32, kind="ExternalOutput").ap())
    build(nc, *args)
    r = _run(nc, [arrays], core_ids=[0])
    return r.results[0]["out_0"]
```
